# Optimizing a Trainium2 kernel written in Bass

```python
import numpy as np
import jax
import jax.numpy as jnp

def _softmax(x, axis=-1):
    return jax.nn.softmax(x, axis=axis)

def _gelu(x):
    return jax.nn.gelu(x, approximate=True)

def _silu(x):
    return jax.nn.silu(x)

def _sigmoid(x):
    return jax.nn.sigmoid(x)

def _layernorm(x, axis=-1, eps=1e-05):
    m = jnp.mean(x, axis=axis, keepdims=True)
    v = jnp.var(x, axis=axis, keepdims=True)
    return (x - m) / jnp.sqrt(v + eps)

def _scatter_add(tgt, idx, src, axis=0):
    return tgt.at[idx].add(src)

def _segment_sum(src, seg, n):
    return jax.ops.segment_sum(src, seg, n)
kernel_name = 'mk_conv_attn_hybrid_d2_conv_nhwc384_r4_0fae6f'

def setup_inputs(seed: int=0):
    np.random.seed(seed)
    _w = jnp.asarray

    def _rec_inputs():
        import jax
        import jax.numpy as jnp
        _gk = jax.random.key(seed)
        x = -0.0005963 + 1.001 * jax.random.normal(jax.random.fold_in(_gk, 1), (8, 32, 32, 96), jnp.float32)
        return x
    x = _rec_inputs()

    def _L0_conv_setup():
        import jax, jax.numpy as jnp
        import numpy as np
        B, H, W, C = (8, 32, 32, 96)
        NH, HD = (6, 16)
        SCALE = HD ** (-0.5)

        def _get_rel_pos(rel_pos, q_size, k_size):
            coords = jnp.arange(q_size)[:, None] - jnp.arange(k_size)[None, :] + (k_size - 1)
            return rel_pos[coords]
        key = jax.random.key(seed)
        ks = jax.random.split(key, 7)
        return {'x': jax.random.normal(ks[0], (B, H, W, C), jnp.float32), 'qkv_w': jax.random.normal(ks[1], (C, 3 * C), jnp.float32) * 0.02, 'qkv_b': jax.random.normal(ks[2], (3 * C,), jnp.float32) * 0.02, 'proj_w': jax.random.normal(ks[3], (C, C), jnp.float32) * 0.02, 'proj_b': jax.random.normal(ks[4], (C,), jnp.float32) * 0.02, 'rel_pos_h': jax.random.normal(ks[5], (2 * H - 1, HD), jnp.float32) * 0.02, 'rel_pos_w': jax.random.normal(ks[6], (2 * W - 1, HD), jnp.float32) * 0.02}
    _L0_conv_all = _L0_conv_setup()
    _L0_conv_in = {k: v for k, v in _L0_conv_all.items() if k in ('qkv_w', 'qkv_b', 'proj_w', 'proj_b', 'rel_pos_h', 'rel_pos_w')}
    del _L0_conv_all

    def _L1_attn_setup():
        import jax, jax.numpy as jnp
        import numpy as np
        import math
        B, T, N_EMBD, N_HEAD = (4, 1024, 96, 6)
        HEAD_DIM = N_EMBD // N_HEAD
        key = jax.random.key(seed)
        k1, k2, k3 = jax.random.split(key, 3)
        x = jax.random.normal(k1, (B, T, N_EMBD), dtype=jnp.float32)
        w_attn = jax.random.normal(k2, (N_EMBD, 3 * N_EMBD), dtype=jnp.float32) * 0.02
        w_proj = jax.random.normal(k3, (N_EMBD, N_EMBD), dtype=jnp.float32) * 0.02
        return {'x': x, 'w_attn': w_attn, 'w_proj': w_proj}
    _L1_attn_all = _L1_attn_setup()
    _L1_attn_in = {k: v for k, v in _L1_attn_all.items() if k in ('w_attn', 'w_proj')}
    del _L1_attn_all

    def _L1_ffn_setup():
        import jax, jax.numpy as jnp
        import numpy as np
        NUM_EXPERTS = 4
        TOP_K = 2
        DIM = 96
        HID = 4 * DIM
        key = jax.random.key(seed)
        ks = jax.random.split(key, 5)
        B, S = (16, 512)
        scale_in = 1.0 / np.sqrt(DIM)
        scale_hid = 1.0 / np.sqrt(HID)
        return {'x': jax.random.normal(ks[0], (B, S, DIM), dtype=jnp.float32), 'gate_w': jax.random.normal(ks[1], (DIM, NUM_EXPERTS), dtype=jnp.float32) * scale_in, 'gate_b': jnp.zeros((NUM_EXPERTS,), dtype=jnp.float32), 'w1': jax.random.normal(ks[2], (NUM_EXPERTS, DIM, HID), dtype=jnp.float32) * scale_in, 'b1': jnp.zeros((NUM_EXPERTS, HID), dtype=jnp.float32), 'w2': jax.random.normal(ks[3], (NUM_EXPERTS, HID, DIM), dtype=jnp.float32) * scale_hid, 'b2': jnp.zeros((NUM_EXPERTS, DIM), dtype=jnp.float32)}
    _L1_ffn_all = _L1_ffn_setup()
    _L1_ffn_in = {k: v for k, v in _L1_ffn_all.items() if k in ('gate_w', 'gate_b', 'w1', 'b1', 'w2', 'b2')}
    del _L1_ffn_all
    return {'x': x, 'L0_conv_qkv_w': _L0_conv_in['qkv_w'], 'L0_conv_qkv_b': _L0_conv_in['qkv_b'], 'L0_conv_proj_w': _L0_conv_in['proj_w'], 'L0_conv_proj_b': _L0_conv_in['proj_b'], 'L0_conv_rel_pos_h': _L0_conv_in['rel_pos_h'], 'L0_conv_rel_pos_w': _L0_conv_in['rel_pos_w'], 'L1_attn_w_attn': _L1_attn_in['w_attn'], 'L1_attn_w_proj': _L1_attn_in['w_proj'], 'L1_ffn_gate_w': _L1_ffn_in['gate_w'], 'L1_ffn_gate_b': _L1_ffn_in['gate_b'], 'L1_ffn_w1': _L1_ffn_in['w1'], 'L1_ffn_b1': _L1_ffn_in['b1'], 'L1_ffn_w2': _L1_ffn_in['w2'], 'L1_ffn_b2': _L1_ffn_in['b2']}

def reference(x, L0_conv_qkv_w, L0_conv_qkv_b, L0_conv_proj_w, L0_conv_proj_b, L0_conv_rel_pos_h, L0_conv_rel_pos_w, L1_attn_w_attn, L1_attn_w_proj, L1_ffn_gate_w, L1_ffn_gate_b, L1_ffn_w1, L1_ffn_b1, L1_ffn_w2, L1_ffn_b2):
    import jax
    import jax.numpy as jnp

    def _L0_conv_ref(x, qkv_w, qkv_b, proj_w, proj_b, rel_pos_h, rel_pos_w):
        import jax, jax.numpy as jnp
        import numpy as np
        B, H, W, C = (8, 32, 32, 96)
        NH, HD = (6, 16)
        SCALE = HD ** (-0.5)

        def _get_rel_pos(rel_pos, q_size, k_size):
            coords = jnp.arange(q_size)[:, None] - jnp.arange(k_size)[None, :] + (k_size - 1)
            return rel_pos[coords]
        b, h, w, c = x.shape
        hw = h * w
        qkv = x.reshape(b, hw, c) @ qkv_w + qkv_b
        qkv = qkv.reshape(b, hw, 3, NH, HD).transpose(2, 0, 3, 1, 4)
        qkv = qkv.reshape(3, b * NH, hw, HD)
        q, k, v = (qkv[0], qkv[1], qkv[2])
        attn = jnp.einsum('bqd,bkd->bqk', q * SCALE, k)
        Rh = _get_rel_pos(rel_pos_h, h, h)
        Rw = _get_rel_pos(rel_pos_w, w, w)
        r_q = q.reshape(b * NH, h, w, HD)
        rel_h = jnp.einsum('bhwc,hkc->bhwk', r_q, Rh)
        rel_w = jnp.einsum('bhwc,wkc->bhwk', r_q, Rw)
        attn = attn.reshape(b * NH, h, w, h, w) + rel_h[:, :, :, :, None] + rel_w[:, :, :, None, :]
        attn = attn.reshape(b * NH, hw, hw)
        attn = jax.nn.softmax(attn, axis=-1)
        out = jnp.einsum('bqk,bkd->bqd', attn, v)
        out = out.reshape(b, NH, h, w, HD).transpose(0, 2, 3, 1, 4).reshape(b, h, w, c)
        return out @ proj_w + proj_b

    def _L1_attn_ref(x, w_attn, w_proj):
        import jax, jax.numpy as jnp
        import numpy as np
        import math
        B, T, N_EMBD, N_HEAD = (4, 1024, 96, 6)
        HEAD_DIM = N_EMBD // N_HEAD
        b, t, c = x.shape
        qkv = x @ w_attn
        q, k, v = jnp.split(qkv, 3, axis=-1)
        q = q.reshape(b, t, N_HEAD, HEAD_DIM)
        k = k.reshape(b, t, N_HEAD, HEAD_DIM)
        v = v.reshape(b, t, N_HEAD, HEAD_DIM)
        scale = 1.0 / math.sqrt(HEAD_DIM)
        att = jnp.einsum('bqhd,bkhd->bhqk', q, k) * scale
        causal = jnp.tril(jnp.ones((t, t), dtype=bool))
        att = jnp.where(causal[None, None], att, jnp.finfo(att.dtype).min)
        att = jax.nn.softmax(att, axis=-1)
        out = jnp.einsum('bhqk,bkhd->bqhd', att, v).reshape(b, t, c)
        return out @ w_proj

    def _L1_ffn_ref(x, gate_w, gate_b, w1, b1, w2, b2):
        import jax, jax.numpy as jnp
        import numpy as np
        NUM_EXPERTS = 4
        TOP_K = 2
        DIM = 96
        HID = 4 * DIM
        scores = jnp.einsum('bsd,de->bse', x, gate_w) + gate_b
        probs = jax.nn.softmax(scores, axis=-1)
        topk_vals, topk_idx = jax.lax.top_k(probs, TOP_K)
        mask = jnp.sum(jax.nn.one_hot(topk_idx, NUM_EXPERTS, dtype=probs.dtype), axis=-2)
        masked = probs * mask
        masked = masked / (jnp.sum(masked, axis=-1, keepdims=True) + 1e-09)
        h = jax.nn.gelu(jnp.einsum('bsd,edh->ebsh', x, w1) + b1[:, None, None, :], approximate=False)
        y = jnp.einsum('ebsh,ehd->ebsd', h, w2) + b2[:, None, None, :]
        out = jnp.einsum('bse,ebsd->bsd', masked, y)
        return out

    def _gn(v, G=32, eps=1e-05):
        B_, H_, W_, C_ = v.shape
        g = v.reshape(B_, H_, W_, G, C_ // G)
        m = jnp.mean(g, axis=(1, 2, 4), keepdims=True)
        s = jnp.var(g, axis=(1, 2, 4), keepdims=True)
        return ((g - m) / jnp.sqrt(s + eps)).reshape(v.shape)

    def _ln_c(v, eps=1e-06):
        m = jnp.mean(v, axis=-1, keepdims=True)
        s = jnp.var(v, axis=-1, keepdims=True)
        return (v - m) / jnp.sqrt(s + eps)

    def _ln_t(v, eps=1e-05):
        m = jnp.mean(v, axis=-1, keepdims=True)
        s = jnp.var(v, axis=-1, keepdims=True)
        return (v - m) / jnp.sqrt(s + eps)

    def _to_tokens(v):
        B_, H_, W_, C_ = v.shape
        return v.reshape(B_, H_ * W_, C_)

    def _from_tokens(t, like):
        return t.reshape(like.shape)
    x = x + _L0_conv_ref(_gn(x), L0_conv_qkv_w, L0_conv_qkv_b, L0_conv_proj_w, L0_conv_proj_b, L0_conv_rel_pos_h, L0_conv_rel_pos_w)
    t = _to_tokens(x)
    t = t + _L1_attn_ref(_ln_t(t), L1_attn_w_attn, L1_attn_w_proj)
    t = t + _L1_ffn_ref(_ln_t(t), L1_ffn_gate_w, L1_ffn_gate_b, L1_ffn_w1, L1_ffn_b1, L1_ffn_w2, L1_ffn_b2)
    x = _from_tokens(t, x)
    return x

_drawn_inputs = setup_inputs


def setup_inputs(seed=0):
    import zlib

    import numpy as np

    out = dict(_drawn_inputs(seed))
    spreads = {'L1_ffn_gate_b': (0.0, 0.1), 'L1_ffn_b1': (0.0, 0.1), 'L1_ffn_b2': (0.0, 0.1)}
    factors = {'L0_conv_qkv_w': 6.966,
     'L0_conv_qkv_b': 3.371,
     'L0_conv_proj_w': 5.133,
     'L0_conv_rel_pos_h': 8.0,
     'L0_conv_rel_pos_w': 8.0,
     'L1_attn_w_attn': 4.666,
     'L1_attn_w_proj': 4.416}
    for name, (base, spread) in spreads.items():
        noise = np.random.default_rng([zlib.crc32(name.encode()), seed]).standard_normal(out[name].shape)
        drawn = base * np.exp(spread * noise) if base else spread * noise
        out[name] = jnp.asarray(drawn.astype(out[name].dtype))
    for name, factor in factors.items():
        out[name] = (out[name] * factor).astype(out[name].dtype)
    return out
```

```python
from contextlib import ExitStack

import concourse.bass as bass
from concourse import mybir

F32 = mybir.dt.float32
F32R = mybir.dt.float32r
BF16 = mybir.dt.bfloat16
ALU = mybir.AluOpType
ACT = mybir.ActivationFunctionType
AX = mybir.AxisListType.X

B, HS, WS, C = 8, 32, 32, 96
T = HS * WS
NH, HD = 6, 16
P = 128
NT = T // P
HALF = 512
NC = T // HALF
PAIRS = NH // 2
NE, HID = 4, 384
HJ = HID // P
GROUP = C // 32
SCALE = HD ** -0.5
BIG = 1.0e30
WIN = 2 * HS - 1
GN_EPS, LN_EPS, GATE_EPS = 1e-5, 1e-5, 1e-9
REL_STEP = 4
REL_FILLS = HS // REL_STEP
ATT_FILLS = NH * NT

Q_SLOTS = (0, 0, 1, 1, 0, 2)
K_SLOTS = (0, 1, 0, 1, 2, 0)

C_ID, C_GRP, C_HOT, C_MQ, C_MK, C_TIE, C_S1, C_S2, C_END = 0, 128, 224, 1248, 1376, 1504, 1520, 1521, 1522

STAGES = ("gn", "qkv0", "rel", "attn0", "proj0", "qkv1", "attn1", "proj1", "ffn")


def max_cols(layer, t, kc):
    return max(0, min(HALF, (t + 1) * P - kc * HALF)) if layer else HALF


MAX_STEPS = [[(h, t, kc) for h in range(NH) for t in range(NT) for kc in range(NC) if max_cols(l, t, kc)]
             for l in (0, 1)]
PER_PAIR = [len(m) // PAIRS for m in MAX_STEPS]

_ATT = {"attn0": 1, "attn1": 1}
_PROJ = {"proj0": 1, "proj1": 1}
INCS = {
    "xt_in": {"gn": 16}, "x0_in": {"gn": 16}, "out_done": {"ffn": 16},
    "gstat": {"gn": 1}, "xnt_gn": {"gn": 1},
    "var_ready": {"gn": 1, **_PROJ}, "ln_var": {"gn": 1, **_PROJ}, "rs0": {"gn": 1, **_PROJ},
    "t_full": {"qkv0": 3, "rel": REL_FILLS, "attn0": ATT_FILLS, "proj0": 2, "qkv1": 3, "attn1": ATT_FILLS,
               "proj1": 2, "ffn": NE * HJ},
    "s_full": {"attn0": len(MAX_STEPS[0]), "attn1": len(MAX_STEPS[1]), "ffn": 2 * NE},
    "m_full": {"gn": 1, "attn0": PAIRS, "attn1": PAIRS, "ffn": 1},
    "y_full": {"ffn": NE},
    "o_free": {s: PAIRS for s in _ATT},
    "lvl1": {"qkv0": 2, "qkv1": 2}, "lvl2": {"qkv0": 2, "qkv1": 2}, "lvl3": {"qkv0": 2, "qkv1": 2},
    "wide3": {"qkv0": 2},
    "spill_q": {"qkv0": 32, "qkv1": 16}, "spill_k": {"qkv0": 32, "qkv1": 16},
    "qr_in": {"qkv0": 96}, "ab_in": {"qkv0": 192}, "l1_in": {"qkv1": 192},
    "rel_lead": {"rel": REL_FILLS},
    "rowmax": {s: PAIRS for s in _ATT},
    "negmax_in": {s: 16 * PAIRS for s in _ATT},
    "p_used": {s: ATT_FILLS for s in _ATT},
    "au_in": {s: 128 * PAIRS for s in _ATT},
    "lnl": _PROJ, "il0": _PROJ, "att_ready": _PROJ, "xn_tok_ready": _PROJ,
    "gate_max_ready": {"ffn": 1}, "gate_exp_ready": {"ffn": 1},
    "dve_chain": {"gn": 8, "proj0": 10, "proj1": 10, "ffn": 12},
}
for _r in "tsmy":
    INCS[f"{_r}_free"] = INCS[f"{_r}_full"]
PER = {s: sum(v.values()) for s, v in INCS.items()}
START = 2


def before(sem, stage):
    return sum(INCS[sem].get(s, 0) for s in STAGES[:STAGES.index(stage)])


def upto(sem, it, stage, n):
    return it * PER[sem] + (START + before(sem, stage) + n)


def t_slot(stage, n):
    return (before("t_full", stage) + n) % 2


def s_bank(stage, n):
    return (before("s_full", stage) + n) % 2


def q_from(layer, kt):
    return kt * P if layer else 0


def build(nc, x_tok, x_t, consts, w_qkv0, b_qkv0, w_p0, b_p0, rel_h, rel_w, w_qkv1, w_p1, gate_w, gate_b,
          w1, b1, w2, b2, out):
    with ExitStack() as ctx:
        def sb(name, shape, dt=F32):
            return ctx.enter_context(nc.sbuf_tensor(name, shape, dt))

        def ps(name, shape):
            return ctx.enter_context(nc.psum_tensor(name, shape, F32))

        sems = {n: ctx.enter_context(nc.semaphore(n)) for n in INCS}
        xt_in = sems["xt_in"]
        x0_in = sems["x0_in"]
        out_done = sems["out_done"]
        gstat = sems["gstat"]
        xnt_gn = sems["xnt_gn"]
        var_ready = sems["var_ready"]
        ln_var = sems["ln_var"]
        rs0 = sems["rs0"]
        t_full = sems["t_full"]
        s_full = sems["s_full"]
        m_full = sems["m_full"]
        y_full = sems["y_full"]
        o_free = sems["o_free"]
        lvl1 = sems["lvl1"]
        lvl2 = sems["lvl2"]
        lvl3 = sems["lvl3"]
        wide3 = sems["wide3"]
        spill_q = sems["spill_q"]
        spill_k = sems["spill_k"]
        qr_in = sems["qr_in"]
        ab_in = sems["ab_in"]
        l1_in = sems["l1_in"]
        rel_lead = sems["rel_lead"]
        rowmax = sems["rowmax"]
        negmax_in = sems["negmax_in"]
        p_used = sems["p_used"]
        au_in = sems["au_in"]
        lnl = sems["lnl"]
        il0 = sems["il0"]
        att_ready = sems["att_ready"]
        xn_tok_ready = sems["xn_tok_ready"]
        gate_max_ready = sems["gate_max_ready"]
        gate_exp_ready = sems["gate_exp_ready"]
        dve_chain = sems["dve_chain"]
        t_free = sems["t_free"]
        s_free = sems["s_free"]
        m_free = sems["m_free"]
        y_free = sems["y_free"]
        const_in = ctx.enter_context(nc.semaphore("const_in"))
        setup = ctx.enter_context(nc.semaphore("setup"))

        cst = sb("cst", [P, C_END])
        ident = cst[:, C_ID:C_ID + P]
        group = cst[0:C, C_GRP:C_GRP + C]
        ident_b = sb("ident_b", [P, P], BF16)
        mask_q = sb("mask_q", [P, P], BF16)
        mask_k = sb("mask_k", [P, P], BF16)
        wqkv = [sb("wqkv0", [C + 1, 3 * C]), sb("wqkv1", [C, 3 * C])]
        wp = [sb("wp0", [C + 1, C]), sb("wp1", [C, C])]
        gw = sb("gw", [C + 1, NE])
        w1s = sb("w1s", [C + 1, NE * HID])
        w2s = sb("w2s", [P, NE * HJ, C])
        b2s = sb("b2s", [C, NE])
        relf = sb("relf", [C, 2, WIN])
        relr = sb("relr", [C, 2, WIN])
        rell = sb("rell", [C, 2, WIN], BF16)
        relt = sb("relt", [C, 2, WIN], BF16)

        x0 = sb("x0", [P, NT, C])
        x1 = sb("x1", [P, NT, C])
        x2 = sb("x2", [P, NT, C])
        xn_tok = sb("xn_tok", [P, NT, C])
        xnt = sb("xnt", [C + 1, T])
        split = sb("split", [C, 2, 3, T], BF16)
        resid = sb("resid", [C, T])
        qr = sb("qr", [C + 1, NH, T], BF16)
        kr = sb("kr", [C + 1, NH, T], BF16)
        qa = sb("qa", [P, NH, T], BF16)
        ka = sb("ka", [P, NH, T], BF16)
        qb = sb("qb", [C + 1, NH, T], F32R)
        kb = sb("kb", [C + 1, NH, T], F32R)
        qb_raw, kb_raw = qb[:, :, :].bitcast(F32), kb[:, :, :].bitcast(F32)
        vs = [sb(f"v{l}", [P, NT, NH, 2 * HD]) for l in (0, 1)]
        probs = sb("probs", [P, 4, T])
        wide = probs[0:C, :, :].bitcast(F32R)
        mx = [sb(f"mx{l}", [P, 2, 2 * NT, NC]) for l in (0, 1)]
        mrow = sb("mrow", [P, 2, 2 * NT])
        negm = [sb("negr", [2 * NT, 2, P], F32R), sb("negb", [2 * NT, 2, P], BF16)]
        negm_raw = [negm[0][:, :, :].bitcast(F32), negm[1]]
        ot = sb("ot", [P, PAIRS, HALF])
        au = sb("au", [C, T])
        lb = sb("lb", [C, T])
        il = sb("il", [C, T])
        att = sb("att", [C + 1, T])
        hbuf = probs
        yt = au
        gs6 = sb("gs6", [C, 2, 6])
        gsm = sb("gsm", [C, 16])
        gst = sb("gst", [C, 2])
        gm = sb("gm", [C, 8])
        st6 = sb("st6", [P, NT, 6])
        sm = sb("sm", [P, 12, NT])
        g4 = sb("g4", [P, 5, NT, NE])
        g16 = sb("g16", [P, 2, NT, NE, NE])
        gden = sb("gden", [P, 4, NT])

        psT = ps("psT", [P, 2, T])
        psS = ps("psS", [P, 2, HALF])
        psOM = ps("psOM", [P, 2, HALF])
        psO, psM = psOM[:, 0, :], psOM[:, 1, :]

        scr = nc.dram_tensor("scr", [C, 2, 3, T], BF16).ap()
        scr32 = nc.dram_tensor("scr32", [C, 4, T], F32).ap()
        scr_d = scr.rearrange("(h d) s l t -> d s l h t", d=HD)
        scr32_d = scr32.rearrange("(h d) s t -> d s h t", d=HD)

        loads = [
            (cst[:, :], consts), (wqkv[0][0:C, :], w_qkv0), (wqkv[0][C:C + 1, :], b_qkv0), (wqkv[1][:, :], w_qkv1),
            (wp[0][0:C, :], w_p0), (wp[0][C:C + 1, :], b_p0), (wp[1][:, :], w_p1), (gw[0:C, :], gate_w),
            (gw[C:C + 1, :], gate_b),
            (w1s[0:C, :].rearrange("c (e h) -> c e h", e=NE), w1.rearrange("e c h -> c e h")),
            (w1s[C:C + 1, :], b1), (w2s[:, :, :], w2.rearrange("e (j p) c -> p (e j) c", p=P)), (b2s[:, :], b2),
            (relf[:, 0, :], rel_h), (relf[:, 1, :], rel_w),
        ]
        n_setup = 30

        block = ctx.enter_context(nc.Block())

        @block.sync
        def _(sp):
            for sem in sems.values():
                sp.sem_inc(sem, START)
            for dst, src in loads:
                sp.dma_start(dst, src).then_inc(const_in, 16)

            def attention(it, layer):
                st = f"attn{layer}"
                for p in range(PAIRS + 1):
                    if p < PAIRS:
                        sp.wait_ge(m_free, upto("m_free", it, st, p + 1))
                        sp.dma_start((qb_raw, qr)[layer][C:C + 1, 2 * p:2 * p + 2, :].rearrange("o h (t q) -> o (h t) q", q=P),
                                     negm_raw[layer][:, p % 2, :]).then_inc(negmax_in, 16)
                    if p >= 1:
                        sp.wait_ge(o_free, upto("o_free", it, st, p))
                        for hh in range(2):
                            for c in range(NC):
                                h, j = 2 * (p - 1) + hh, 32 * (2 * hh + c)
                                rows, cols = slice(h * HD, (h + 1) * HD), slice(c * HALF, (c + 1) * HALF)
                                sp.dma_start(au[rows, cols], ot[j:j + HD, p - 1, :]).then_inc(au_in, 16)
                                sp.dma_start(lb[rows, cols],
                                             ot[j + HD:j + 2 * HD, p - 1, :]).then_inc(au_in, 16)

            with sp.Fori(0, B) as it:
                sp.wait_ge(t_full, upto("t_full", it, "gn", 0))
                sp.wait_ge(y_full, upto("y_full", it, "gn", 0))
                sp.dma_start(xnt[0:C, :], x_t[it]).then_inc(xt_in, 16)
                sp.wait_ge(s_free, upto("s_free", it, "gn", 0))
                sp.dma_start(x0[:, :, :], x_tok[it]).then_inc(x0_in, 16)

                for s, spill in ((0, "spill_q"), (1, "spill_k")):
                    sp.wait_ge(lvl3, upto("lvl3", it, "qkv0", s + 1))
                    sp.dma_start(scr[:, s], split[:, s]).then_inc(sems[spill], 16)
                    sp.wait_ge(wide3, upto("wide3", it, "qkv0", s + 1))
                    sp.dma_start(scr32[:, 2 * s:2 * s + 2], probs[0:C, 2 * s:2 * s + 2, :]).then_inc(sems[spill], 16)
                sp.wait_ge(spill_q, upto("spill_q", it, "qkv0", 32))
                for n, l in enumerate(Q_SLOTS):
                    sp.dma_start(qr[n * HD:(n + 1) * HD, :, :], scr_d[:, 0, l]).then_inc(qr_in, 16)
                for n, l in enumerate(Q_SLOTS[:4]):
                    sp.dma_start(qa[n * HD:(n + 1) * HD, :, :], scr_d[:, 0, l]).then_inc(ab_in, 16)
                for n in range(2):
                    sp.dma_start(qb_raw[64 + n * HD:64 + (n + 1) * HD, :, :], scr32_d[:, n]).then_inc(ab_in, 16)
                sp.wait_ge(spill_k, upto("spill_k", it, "qkv0", 32))
                for n, l in enumerate(K_SLOTS[:4]):
                    sp.dma_start(ka[n * HD:(n + 1) * HD, :, :], scr_d[:, 1, l]).then_inc(ab_in, 16)
                for n in range(2):
                    sp.dma_start(kb_raw[64 + n * HD:64 + (n + 1) * HD, :, :], scr32_d[:, 3 - n]).then_inc(ab_in, 16)
                attention(it, 0)

                for s, spill in ((0, "spill_q"), (1, "spill_k")):
                    sp.wait_ge(lvl3, upto("lvl3", it, "qkv1", s + 1))
                    sp.dma_start(scr[:, s], split[:, s]).then_inc(sems[spill], 16)
                sp.wait_ge(spill_q, upto("spill_q", it, "qkv1", 16))
                for n, l in enumerate(Q_SLOTS):
                    sp.dma_start(qr[n * HD:(n + 1) * HD, :, :], scr_d[:, 0, l]).then_inc(l1_in, 16)
                sp.wait_ge(spill_k, upto("spill_k", it, "qkv1", 16))
                for n, l in enumerate(K_SLOTS):
                    sp.dma_start(kr[n * HD:(n + 1) * HD, :, :], scr_d[:, 1, l]).then_inc(l1_in, 16)
                attention(it, 1)
                sp.wait_ge(y_free, upto("y_free", it, "ffn", NE))
                sp.dma_start(out[it], x2[:, :, :]).then_inc(out_done, 16)
            sp.wait_ge(out_done, START + 16 * B)

        @block.tensor
        def _(pe):
            mm = nc.tensor.matmul

            def take_t(it, stage, n):
                pe.wait_ge(t_free, upto("t_free", it, stage, n - 1))
                return psT[:, t_slot(stage, n), :]

            def project(it, layer):
                st, k, w = f"qkv{layer}", C + 1 - layer, wqkv[layer]
                for s in range(2):
                    o = take_t(it, st, s)
                    for c in range(NC):
                        last = mm(o[0:C, c * HALF:(c + 1) * HALF], w[0:k, s * C:(s + 1) * C],
                                  xnt[0:k, c * HALF:(c + 1) * HALF], start=True, stop=True)
                    last.then_inc(t_full, 1)
                o = take_t(it, st, 2)
                for t in range(NT):
                    a = (t // 4) * HALF + (t % 4) * C
                    last = mm(o[:, a:a + C], xnt[0:k, t * P:(t + 1) * P], w[0:k, 2 * C:3 * C], start=True, stop=True)
                last.then_inc(t_full, 1)

            def bias(it):
                pe.wait_ge(qr_in, upto("qr_in", it, "qkv0", 96))
                q_cols = qr[0:C, :, :].rearrange("c h (a b) -> c h a b", b=WS)
                for g in range(REL_FILLS):
                    o = take_t(it, "rel", g)
                    for i in range(REL_STEP):
                        r = REL_STEP * g + i
                        window = slice(HS - 1 - r, 2 * HS - 1 - r)
                        mm(o[0:HS, 256 * i:256 * i + NH * WS], relt[:, 0, window], qr[0:C, :, r * WS:(r + 1) * WS],
                           start=True, stop=True)
                        last = mm(o[HS:2 * HS, 256 * i:256 * i + NH * HS], relt[:, 1, window], q_cols[:, :, :, r],
                                  start=True, stop=True)
                    last.then_inc(t_full, 1)

            def attention(it, layer):
                st, v = f"attn{layer}", vs[layer]

                def max_scores(fill):
                    h, t, kc = MAX_STEPS[layer][fill]
                    n = max_cols(layer, t, kc)
                    pe.wait_ge(s_free, upto("s_free", it, st, fill - 1))
                    bank = psS[:, s_bank(st, fill), :]
                    q, k, rows = ((qa, ka, P), (qr, kr, C))[layer]
                    diagonal = layer == 1 and (t + 1) * P <= (kc + 1) * HALF
                    last = mm(bank[:, 0:n], q[0:rows, h, t * P:(t + 1) * P], k[0:rows, h, kc * HALF:kc * HALF + n],
                              start=True, stop=not diagonal)
                    if diagonal:
                        last = mm(bank[:, n - P:n], ident_b[:, :], mask_q[:, :], start=False, stop=True)
                    last.then_inc(s_full, 1)

                def transpose_max(p):
                    pe.wait_ge(rowmax, upto("rowmax", it, st, p + 1))
                    pe.wait_ge(m_free, upto("m_free", it, st, p))
                    mm(psM[0:2 * NT, 0:P], mrow[:, p % 2, :], ident, is_transpose=True, start=True,
                       stop=True).then_inc(m_full, 1)

                def scores(p, kt, hh):
                    h, q0, ks = 2 * p + hh, q_from(layer, kt), slice(kt * P, (kt + 1) * P)
                    o = take_t(it, st, (p * NT + kt) * 2 + hh)
                    for c in range(NC):
                        a, b = max(q0, c * HALF), (c + 1) * HALF
                        if a >= b:
                            continue
                        if layer == 0:
                            mm(o[:, a:b], ka[:, h, ks], qa[:, h, a:b], start=True, stop=False)
                            last = mm(o[:, a:b], kb[:, h, ks], qb[:, h, a:b], start=False, stop=True)
                        else:
                            last = mm(o[:, a:b], kr[:, h, ks], qr[:, h, a:b], start=True, stop=a != q0)
                            if a == q0:
                                last = mm(o[:, a:a + P], ident_b[:, :], mask_k[:, :], start=False, stop=True)
                    last.then_inc(t_full, 1)

                def values(p, kt):
                    q0 = q_from(layer, kt)
                    if kt == 0:
                        pe.wait_ge(o_free, upto("o_free", it, st, p))
                    for hh in range(2):
                        pe.wait_ge(t_free, upto("t_free", it, st, (p * NT + kt) * 2 + hh + 1))
                        for c in range(NC):
                            a, j = max(q0, c * HALF), 32 * (2 * hh + c)
                            if a >= (c + 1) * HALF:
                                continue
                            end = NT if layer == 0 else (c + 1) * HALF // P
                            last = mm(psO[j:j + 2 * HD, a - c * HALF:HALF], v[:, kt, 2 * p + hh, :],
                                      probs[:, (2 * kt + hh) % 4, a:(c + 1) * HALF], start=kt == 0, stop=kt == end - 1)
                        last.then_inc(p_used, 1)

                n = PER_PAIR[layer]
                for fill in range(n):
                    max_scores(fill)
                transpose_max(0)
                for p in range(PAIRS):
                    ahead = range((p + 1) * n, (p + 2) * n) if p + 1 < PAIRS else ()
                    cut = [len(ahead) * i // (2 * NT) for i in range(2 * NT + 1)]
                    pe.wait_ge(negmax_in, upto("negmax_in", it, st, 16 * (p + 1)))
                    for kt in range(NT):
                        for hh in range(2):
                            scores(p, kt, hh)
                            if hh == 1 and kt >= 1:
                                values(p, kt - 1)
                            for fill in ahead[cut[2 * kt + hh]:cut[2 * kt + hh + 1]]:
                                max_scores(fill)
                    values(p, NT - 1)
                    if p + 1 < PAIRS:
                        transpose_max(p + 1)

            def out_project(it, layer):
                st, k = f"proj{layer}", C + 1 - layer
                pe.wait_ge(att_ready, upto("att_ready", it, st, 1))
                o = take_t(it, st, 0)
                for t in range(NT):
                    a = (t // 4) * HALF + (t % 4) * C
                    last = mm(o[:, a:a + C], att[0:k, t * P:(t + 1) * P], wp[layer][0:k, :], start=True, stop=True)
                last.then_inc(t_full, 1)
                pe.wait_ge(xn_tok_ready, upto("xn_tok_ready", it, st, 1))
                o = take_t(it, st, 1)
                for t in range(NT):
                    last = mm(o[0:C, t * P:(t + 1) * P], xn_tok[:, t, :], ident, is_transpose=True, start=True,
                              stop=True)
                last.then_inc(t_full, 1)

            def experts(it):
                pe.wait_ge(m_free, upto("m_free", it, "ffn", 0))
                for t in range(NT):
                    last = mm(psM[:, t * NE:(t + 1) * NE], xnt[:, t * P:(t + 1) * P], gw[:, :], start=True, stop=True)
                last.then_inc(m_full, 1)
                for x in range(NE):
                    for j in range(HJ):
                        o = take_t(it, "ffn", HJ * x + j)
                        a = x * HID + j * P
                        for c in range(NC):
                            last = mm(o[:, c * HALF:(c + 1) * HALF], w1s[:, a:a + P],
                                      xnt[:, c * HALF:(c + 1) * HALF], start=True, stop=True)
                        last.then_inc(t_full, 1)
                    for c in range(NC):
                        pe.wait_ge(s_free, upto("s_free", it, "ffn", 2 * x + c - 1))
                        for j in range(HJ):
                            pe.wait_ge(t_free, upto("t_free", it, "ffn", HJ * x + j + 1))
                            last = mm(psS[0:C, s_bank("ffn", 2 * x + c), :], w2s[:, x * HJ + j, :],
                                      hbuf[:, j, c * HALF:(c + 1) * HALF], start=j == 0, stop=j == HJ - 1)
                        last.then_inc(s_full, 1)
                    pe.wait_ge(s_free, upto("s_free", it, "ffn", 2 * x + 2))
                    pe.wait_ge(y_free, upto("y_free", it, "ffn", x))
                    if x == 0:
                        pe.wait_ge(m_free, upto("m_free", it, "ffn", 1))
                        pe.wait_ge(o_free, upto("o_free", it, "ffn", 0))
                    for t in range(NT):
                        last = mm(psOM[:, t // 4, (t % 4) * C:(t % 4 + 1) * C], yt[:, t * P:(t + 1) * P],
                                  ident[0:C, 0:C], is_transpose=True, start=True, stop=True)
                    last.then_inc(y_full, 1)

            pe.wait_ge(const_in, 16 * len(loads))
            pe.wait_ge(setup, n_setup)
            with pe.Fori(0, B) as it:
                pe.wait_ge(gstat, upto("gstat", it, "gn", 1))
                pe.wait_ge(y_free, upto("y_free", it, "gn", 0))
                mm(psM[0:C, 0:2], group, gst[:, :], start=True, stop=True).then_inc(m_full, 1)
                pe.wait_ge(xnt_gn, upto("xnt_gn", it, "gn", 1))
                project(it, 0)
                bias(it)
                pe.wait_ge(ab_in, upto("ab_in", it, "qkv0", 192))
                pe.wait_ge(t_free, upto("t_free", it, "rel", REL_FILLS))
                attention(it, 0)
                out_project(it, 0)
                pe.wait_ge(t_free, upto("t_free", it, "proj0", 2))
                project(it, 1)
                pe.wait_ge(l1_in, upto("l1_in", it, "qkv1", 192))
                pe.wait_ge(t_free, upto("t_free", it, "qkv1", 3))
                attention(it, 1)
                out_project(it, 1)
                pe.wait_ge(t_free, upto("t_free", it, "proj1", 2))
                experts(it)

        def rel_views(dst, base, g, o):
            o = o.rearrange("p (i r) -> p i r", r=256)[:, :, 0:NH * HS]
            r = slice(REL_STEP * g, REL_STEP * (g + 1))
            return ((dst[base:base + HS].rearrange("p h (a b) -> p a h b", b=WS)[:, r],
                     o[0:HS].rearrange("p i (h b) -> p i h b", h=NH)),
                    (dst[base + HS:base + 2 * HS].rearrange("p h (a b) -> p h a b", b=WS)[:, :, :, r],
                     o[HS:2 * HS].rearrange("p i (h a) -> p h a i", h=NH)))

        @block.scalar
        def _(act):
            A = nc.scalar.activation

            def rstd_guess(it, stage, v, lnv, y):
                act.wait_ge(var_ready, upto("var_ready", it, stage, 1))
                A(lnv, v, ACT.Ln).then_inc(ln_var, 1)
                act.wait_ge(ln_var, upto("ln_var", it, stage, 1))
                A(y, lnv, ACT.Exp, scale=-0.5).then_inc(rs0, 1)

            def split_levels(it, layer):
                st = f"qkv{layer}"
                act.wait_ge(spill_q, upto("spill_q", it, st, 0))
                act.wait_ge(spill_k, upto("spill_k", it, st, 0))
                for s in range(2):
                    act.wait_ge(t_full, upto("t_full", it, st, s + 1))
                    A(split[:, s, 0, :], psT[0:C, t_slot(st, s), :], ACT.Copy,
                      scale=(1.0, SCALE)[s]).then_inc(lvl1, 1)
                for s in range(2):
                    act.wait_ge(t_free, upto("t_free", it, st, s + 1))
                    A(split[:, s, 1, :], resid[:, :], ACT.Copy).then_inc(lvl2, 1)
                    if layer == 0:
                        act.wait_ge(lvl1, upto("lvl1", it, st, s + 1))
                        A(wide[:, 2 * s, :], split[:, s, 0, :], ACT.Copy)
                act.wait_ge(t_full, upto("t_full", it, st, 3))
                o = psT[:, t_slot(st, 2), :].rearrange("p (b r) -> p b r", b=2)
                for b in range(2):
                    last = A(vs[layer][:, 4 * b:4 * b + 4, :, 0:HD],
                             o[:, b, 0:4 * C].rearrange("p (t h d) -> p t h d", t=4, h=NH), ACT.Copy)
                last.then_inc(t_free, 1)
                if layer == 0:
                    for s in range(2):
                        act.wait_ge(lvl3, upto("lvl3", it, st, s + 1))
                        A(wide[:, 2 * s + 1, :], split[:, s, 2, :], ACT.Copy).then_inc(wide3, 1)

            def attention(it, layer):
                st = f"attn{layer}"

                def neg_max(p):
                    act.wait_ge(m_full, upto("m_full", it, st, p + 1))
                    act.wait_ge(negmax_in, upto("negmax_in", it, st, 16 * max(p - 1, 0)))
                    A(negm[layer][:, p % 2, :], psM[0:2 * NT, 0:P], ACT.Copy, scale=-1.0).then_inc(m_free, 1)

                def evacuate(p):
                    act.wait_ge(p_used, upto("p_used", it, st, 2 * NT * (p + 1)))
                    act.wait_ge(au_in, upto("au_in", it, st, 0))
                    A(ot[:, p, :], psO, ACT.Copy).then_inc(o_free, 1)

                neg_max(0)
                for p in range(PAIRS):
                    for kt in range(NT):
                        for hh in range(2):
                            n = (p * NT + kt) * 2 + hh
                            act.wait_ge(t_full, upto("t_full", it, st, n + 1))
                            act.wait_ge(p_used, upto("p_used", it, st, max(n - 3, 0)))
                            q0 = q_from(layer, kt)
                            A(probs[:, n % 4, q0:T], psT[:, t_slot(st, n), q0:T], ACT.Exp).then_inc(t_free, 1)
                        if kt == 0 and p >= 1:
                            evacuate(p - 1)
                    if p + 1 < PAIRS:
                        neg_max(p + 1)
                evacuate(PAIRS - 1)

            def normalise(it, layer):
                st = f"proj{layer}"
                act.wait_ge(au_in, upto("au_in", it, f"attn{layer}", 128 * PAIRS))
                A(il[:, :], lb[:, :], ACT.Ln).then_inc(lnl, 1)
                act.wait_ge(lnl, upto("lnl", it, st, 1))
                A(il[:, :], il[:, :], ACT.Exp, scale=-1.0).then_inc(il0, 1)
                rstd_guess(it, st, sm[:, 5, :], sm[:, 6, :], sm[:, 7, :])
                act.wait_ge(t_full, upto("t_full", it, st, 2))
                A(xnt[0:C, :], psT[0:C, t_slot(st, 1), :], ACT.Copy).then_inc(t_free, 1)

            act.wait_ge(const_in, 16 * len(loads))
            act.wait_ge(setup, n_setup)
            with act.Fori(0, B) as it:
                rstd_guess(it, "gn", gm[:, 3:4], gm[:, 4:5], gm[:, 5:6])
                split_levels(it, 0)
                for g in range(REL_FILLS):
                    act.wait_ge(t_full, upto("t_full", it, "rel", g + 1))
                    rows, cols = rel_views(qa, 64, g, psT[:, t_slot("rel", g), :])
                    A(rows[0], rows[1], ACT.Copy)
                    A(cols[0], cols[1], ACT.Copy).then_inc(rel_lead, 1)
                attention(it, 0)
                normalise(it, 0)
                split_levels(it, 1)
                attention(it, 1)
                normalise(it, 1)
                act.wait_ge(gate_max_ready, upto("gate_max_ready", it, "ffn", 1))
                A(g4[:, 1], g4[:, 0], ACT.Exp).then_inc(gate_exp_ready, 1)
                for x in range(NE):
                    act.wait_ge(s_full, upto("s_full", it, "ffn", 2 * x))
                    for j in range(HJ):
                        act.wait_ge(t_full, upto("t_full", it, "ffn", HJ * x + j + 1))
                        A(hbuf[:, j, :], psT[:, t_slot("ffn", HJ * x + j), :], ACT.Gelu).then_inc(t_free, 1)

        @block.vector
        def _(dve):
            V = nc.vector
            done = [0]

            def ready(ins):
                done[0] += 1
                ins.then_inc(setup, 1)
                dve.wait_ge(setup, done[0])

            dve.wait_ge(const_in, 16 * len(loads))
            hot = cst[0:2 * HS, C_HOT:C_HOT + T]
            ready(V.tensor_copy(ident_b[:, :], ident))
            ready(V.tensor_copy(mask_q[:, :], cst[:, C_MQ:C_MQ + P]))
            ready(V.tensor_copy(mask_k[:, :], cst[:, C_MK:C_MK + P]))
            for h in range(NH):
                ready(V.tensor_copy(ka[64:128, h, :], hot))
                ready(V.tensor_copy(kb[0:64, h, :], hot))
            for ones in (kr[C:C + 1, :, :], kb[C:C + 1, :, :].bitcast(F32), xnt[C:C + 1, :], att[C:C + 1, :],
                         vs[0][:, :, :, HD:2 * HD], vs[1][:, :, :, HD:2 * HD]):
                ready(V.memset(ones, 1.0))
            ready(V.memset(mx[0][:, :, :, :], -BIG))
            ready(V.memset(mx[1][:, :, :, :], -BIG))
            ready(V.tensor_copy(rell[:, :, :], relf[:, :, :]))
            ready(V.scalar_tensor_tensor(out=relr[:, :, :], in0=rell[:, :, :], scalar=cst[0:C, C_S1:C_S1 + 1],
                                         in1=relf[:, :, :], op0=ALU.mult, op1=ALU.add))
            ready(V.tensor_copy(rell[:, :, :], relr[:, :, :]))
            ready(V.scalar_tensor_tensor(out=relt[:, :, :], in0=rell[:, :, :], scalar=cst[0:C, C_S2:C_S2 + 1],
                                         in1=relr[:, :, :], op0=ALU.mult, op1=ALU.add))
            while done[0] < n_setup:
                ready(V.memset(gden[:, 3, :], 1.0))
            assert done[0] == n_setup, done[0]

            with dve.Fori(0, B) as it:
                count = {}

                def link(stage, ins):
                    count[stage] = count.get(stage, 0) + 1
                    ins.then_inc(dve_chain, 1)
                    dve.wait_ge(dve_chain, upto("dve_chain", it, stage, count[stage]))

                def newton(stage, v, y, tmp, out):
                    dve.wait_ge(rs0, upto("rs0", it, stage, 1))
                    link(stage, V.tensor_tensor(tmp, y, y, ALU.mult))
                    link(stage, V.tensor_tensor(tmp, tmp, v, ALU.mult))
                    link(stage, V.tensor_scalar(tmp, tmp, -0.5, 1.5, ALU.mult, ALU.add))
                    link(stage, V.tensor_tensor(out, y, tmp, ALU.mult))

                def group_norm():
                    st = "gn"
                    dve.wait_ge(xt_in, upto("xt_in", it, st, 16))
                    for c in range(NC):
                        ins = V.bn_stats(gs6[:, c, :], xnt[0:C, c * HALF:(c + 1) * HALF])
                    link(st, ins)
                    means = gs6[:, :, :].rearrange("p c (k s) -> p (c k) s", s=3)[:, :, 1]
                    sqs = gs6[:, :, :].rearrange("p c (k s) -> p (c k) s", s=3)[:, :, 2]
                    link(st, V.tensor_tensor(gsm[:, 0:4], means, means, ALU.mult))
                    V.reduce_sum(gst[:, 0:1], means, AX)
                    V.reduce_sum(gsm[:, 4:5], gsm[:, 0:4], AX)
                    link(st, V.reduce_sum(gsm[:, 5:6], sqs, AX))
                    V.scalar_tensor_tensor(out=gst[:, 1:2], in0=gsm[:, 5:6], scalar=4.0 / T, in1=gsm[:, 4:5],
                                           op0=ALU.mult, op1=ALU.add).then_inc(gstat, 1)
                    dve.wait_ge(m_full, upto("m_full", it, st, 1))
                    V.tensor_scalar(gm[:, 0:2], psM[0:C, 0:2], 0.25, None, ALU.mult).then_inc(m_free, 1)
                    dve.wait_ge(m_free, upto("m_free", it, st, 1))
                    link(st, V.scalar_tensor_tensor(out=gm[:, 2:3], in0=gm[:, 0:1], scalar=gm[:, 0:1], in1=gm[:, 1:2],
                                                    op0=ALU.mult, op1=ALU.subtract))
                    V.tensor_scalar(gm[:, 3:4], gm[:, 2:3], -1.0, GN_EPS, ALU.mult, ALU.add).then_inc(var_ready, 1)
                    newton(st, gm[:, 3:4], gm[:, 5:6], gm[:, 6:7], gm[:, 7:8])
                    V.tensor_scalar(xnt[0:C, :], xnt[0:C, :], gm[:, 0:1], gm[:, 7:8], ALU.subtract,
                                    ALU.mult).then_inc(xnt_gn, 1)

                def residuals(layer):
                    st = f"qkv{layer}"
                    for s in range(2):
                        dve.wait_ge(lvl1, upto("lvl1", it, st, s + 1))
                        if s == 1:
                            dve.wait_ge(lvl3, upto("lvl3", it, st, 1))
                        V.scalar_tensor_tensor(out=resid[:, :], in0=psT[0:C, t_slot(st, s), :],
                                               scalar=(1.0, SCALE)[s], in1=split[:, s, 0, :], op0=ALU.mult,
                                               op1=ALU.subtract).then_inc(t_free, 1)
                        dve.wait_ge(lvl2, upto("lvl2", it, st, s + 1))
                        V.tensor_tensor(split[:, s, 2, :], resid[:, :], split[:, s, 1, :],
                                        ALU.subtract).then_inc(lvl3, 1)

                def bias_rest():
                    for g in range(REL_FILLS):
                        dve.wait_ge(rel_lead, upto("rel_lead", it, "rel", g + 1))
                        o = psT[:, t_slot("rel", g), :]
                        for lead, rest in zip(rel_views(qa, 64, g, o), rel_views(qb, 0, g, o)):
                            ins = V.tensor_tensor(rest[0], rest[1], lead[0], ALU.subtract)
                        ins.then_inc(t_free, 1)

                def maxima(layer):
                    st = f"attn{layer}"
                    for fill, (h, t, kc) in enumerate(MAX_STEPS[layer]):
                        dve.wait_ge(s_full, upto("s_full", it, st, fill + 1))
                        p = h // 2
                        V.reduce_max(mx[layer][:, p % 2, (h % 2) * NT + t, kc:kc + 1],
                                     psS[:, s_bank(st, fill), 0:max_cols(layer, t, kc)], AX).then_inc(s_free, 1)
                        if (fill + 1) % PER_PAIR[layer] == 0:
                            dve.wait_ge(s_free, upto("s_free", it, st, fill + 1))
                            dve.wait_ge(m_full, upto("m_full", it, st, max(p - 1, 0)))
                            V.tensor_tensor(mrow[:, p % 2, :], mx[layer][:, p % 2, :, 0], mx[layer][:, p % 2, :, 1],
                                            ALU.max).then_inc(rowmax, 1)

                def normalise(layer, res, new):
                    st = f"proj{layer}"
                    dve.wait_ge(il0, upto("il0", it, st, 1))
                    link(st, V.tensor_tensor(lb[:, :], lb[:, :], il[:, :], ALU.mult))
                    link(st, V.scalar_tensor_tensor(out=il[:, :], in0=lb[:, :], scalar=2.0, in1=il[:, :],
                                                    op0=ALU.subtract, op1=ALU.mult))
                    V.scalar_tensor_tensor(out=att[0:C, :], in0=il[:, :], scalar=-1.0, in1=au[:, :], op0=ALU.mult,
                                           op1=ALU.mult).then_inc(att_ready, 1)
                    if layer == 0:
                        dve.wait_ge(x0_in, upto("x0_in", it, "gn", 16))
                    else:
                        dve.wait_ge(out_done, upto("out_done", it, st, 0))
                    dve.wait_ge(t_full, upto("t_full", it, st, 1))
                    o = psT[:, t_slot(st, 0), :].rearrange("p (b r) -> p b r", b=2)[:, :, 0:4 * C]
                    V.tensor_tensor(new[:, :, :].rearrange("p (b t) c -> p b (t c)", b=2), o,
                                    res[:, :, :].rearrange("p (b t) c -> p b (t c)", b=2),
                                    ALU.add).then_inc(t_free, 1)
                    dve.wait_ge(t_free, upto("t_free", it, st, 1))
                    for t in range(NT):
                        ins = V.bn_stats(st6[:, t, :], new[:, t, :])
                    link(st, ins)
                    me, ve, mo, vo = (st6[:, :, k] for k in (1, 2, 4, 5))
                    V.tensor_tensor(sm[:, 0, :], me, mo, ALU.add)
                    V.tensor_tensor(sm[:, 1, :], me, mo, ALU.subtract)
                    link(st, V.tensor_tensor(sm[:, 2, :], ve, vo, ALU.add))
                    V.tensor_scalar(sm[:, 8, :], sm[:, 0, :], 0.5, None, ALU.mult)
                    link(st, V.scalar_tensor_tensor(out=sm[:, 3, :], in0=sm[:, 1, :], scalar=0.25, in1=sm[:, 1, :],
                                                    op0=ALU.mult, op1=ALU.mult))
                    link(st, V.scalar_tensor_tensor(out=sm[:, 4, :], in0=sm[:, 2, :], scalar=1.0 / C, in1=sm[:, 3, :],
                                                    op0=ALU.mult, op1=ALU.add))
                    V.tensor_scalar(sm[:, 5, :], sm[:, 4, :], LN_EPS, None, ALU.add).then_inc(var_ready, 1)
                    newton(st, sm[:, 5, :], sm[:, 7, :], sm[:, 9, :], sm[:, 10, :])
                    for t in range(NT):
                        ins = V.tensor_scalar(xn_tok[:, t, :], new[:, t, :], sm[:, 8, t:t + 1], sm[:, 10, t:t + 1],
                                              ALU.subtract, ALU.mult)
                    ins.then_inc(xn_tok_ready, 1)

                def gates():
                    st = "ffn"
                    dve.wait_ge(m_full, upto("m_full", it, st, 1))
                    s = psM[:, 0:NT * NE].rearrange("p (t x) -> p t x", x=NE)

                    def over(row):
                        return row.unsqueeze(2).to_broadcast([P, NT, NE])

                    link(st, V.reduce_max(gden[:, 0, :], s, AX))
                    V.tensor_tensor(g4[:, 0], s, over(gden[:, 0, :]), ALU.subtract).then_inc(gate_max_ready, 1)
                    dve.wait_ge(gate_exp_ready, upto("gate_exp_ready", it, st, 1))
                    link(st, V.reduce_sum(gden[:, 1, :], g4[:, 1], AX))
                    link(st, V.reciprocal(gden[:, 2, :], gden[:, 1, :]))
                    link(st, V.tensor_tensor(g4[:, 2], g4[:, 1], over(gden[:, 2, :]), ALU.mult))
                    shape = [P, NT, NE, NE]
                    mine = g4[:, 2].unsqueeze(3).to_broadcast(shape)
                    other = g4[:, 2].unsqueeze(2).to_broadcast(shape)
                    V.tensor_tensor(g16[:, 0], other, mine, ALU.is_gt)
                    link(st, V.tensor_tensor(g16[:, 1], other, mine, ALU.is_equal))
                    tie = cst[:, C_TIE:C_TIE + NE * NE].rearrange("p (i j) -> p i j", j=NE).unsqueeze(1).to_broadcast(shape)
                    link(st, V.tensor_tensor(g16[:, 1], g16[:, 1], tie, ALU.mult))
                    link(st, V.tensor_tensor(g16[:, 0], g16[:, 0], g16[:, 1], ALU.add))
                    link(st, V.reduce_sum(g4[:, 3], g16[:, 0], AX))
                    link(st, V.scalar_tensor_tensor(out=g4[:, 4], in0=g4[:, 3], scalar=1.5, in1=g4[:, 2],
                                                    op0=ALU.is_lt, op1=ALU.mult))
                    link(st, V.reduce_sum(gden[:, 0, :], g4[:, 4], AX))
                    link(st, V.tensor_scalar(gden[:, 1, :], gden[:, 0, :], GATE_EPS, None, ALU.add))
                    link(st, V.reciprocal(gden[:, 2, :], gden[:, 1, :]))
                    V.tensor_tensor(g4[:, 0], g4[:, 4], over(gden[:, 2, :]), ALU.mult).then_inc(m_free, 1)

                def experts():
                    st = "ffn"
                    dve.wait_ge(m_free, upto("m_free", it, st, 1))
                    for x in range(NE):
                        dve.wait_ge(y_full, upto("y_full", it, st, x))
                        for c in range(NC):
                            dve.wait_ge(s_full, upto("s_full", it, st, 2 * x + c + 1))
                            V.tensor_scalar(yt[:, c * HALF:(c + 1) * HALF], psS[0:C, s_bank(st, 2 * x + c), :],
                                            b2s[:, x:x + 1], None, ALU.add).then_inc(s_free, 1)
                        dve.wait_ge(y_full, upto("y_full", it, st, x + 1))
                        dve.wait_ge(y_free, upto("y_free", it, st, x))
                        for t in range(NT):
                            ins = V.scalar_tensor_tensor(out=x2[:, t, :], in0=psOM[:, t // 4, (t % 4) * C:(t % 4 + 1) * C],
                                                         scalar=g4[:, 0, t, x:x + 1], in1=x2[:, t, :],
                                                         op0=ALU.mult, op1=ALU.add)
                        ins.then_inc(y_free, 1)

                group_norm()
                residuals(0)
                bias_rest()
                maxima(0)
                normalise(0, x0, x1)
                residuals(1)
                maxima(1)
                normalise(1, x1, x2)
                gates()
                experts()
                for stage, n in count.items():
                    assert INCS["dve_chain"][stage] == n, (stage, n)




def _constants(np):
    c = np.zeros((P, C_END), np.float32)
    i, j = np.arange(P)[:, None], np.arange(P)[None, :]
    c[:, C_ID:C_ID + P] = i == j
    g = np.arange(C) // GROUP
    c[0:C, C_GRP:C_GRP + C] = (g[:, None] == g[None, :]) / GROUP
    key = np.arange(T)
    c[0:HS, C_HOT:C_HOT + T] = key[None, :] // WS == np.arange(HS)[:, None]
    c[HS:2 * HS, C_HOT:C_HOT + T] = key[None, :] % WS == np.arange(WS)[:, None]
    c[:, C_MQ:C_MQ + P] = np.where(j > i, -BIG, 0)
    c[:, C_MK:C_MK + P] = np.where(i > j, -BIG, 0)
    x = np.arange(NE)
    c[:, C_TIE:C_TIE + NE * NE] = (x[None, :] < x[:, None]).reshape(1, -1)
    level = np.repeat(K_SLOTS, HD)
    c[0:C, C_S1] = np.where(level >= 1, -1, 0)
    c[0:C, C_S2] = np.where(level >= 2, -1, 0)
    return c


def kernel(x, L0_conv_qkv_w, L0_conv_qkv_b, L0_conv_proj_w, L0_conv_proj_b, L0_conv_rel_pos_h, L0_conv_rel_pos_w,
           L1_attn_w_attn, L1_attn_w_proj, L1_ffn_gate_w, L1_ffn_gate_b, L1_ffn_w1, L1_ffn_b1, L1_ffn_w2, L1_ffn_b2):
    import numpy as np
    import concourse.bacc as bacc
    from concourse.bass_utils import run_bass_kernel_spmd as run

    def table(r):
        return np.tile(np.asarray(r)[::-1].T, (len(K_SLOTS), 1))

    x = np.asarray(x)
    arrays = {
        "x_tok": x.reshape(B, NT, P, C).transpose(0, 2, 1, 3),
        "x_t": x.reshape(B, T, C).transpose(0, 2, 1),
        "consts": _constants(np),
        "w_qkv0": L0_conv_qkv_w, "b_qkv0": np.asarray(L0_conv_qkv_b)[None, :],
        "w_p0": L0_conv_proj_w, "b_p0": np.asarray(L0_conv_proj_b)[None, :],
        "rel_h": table(L0_conv_rel_pos_h), "rel_w": table(L0_conv_rel_pos_w),
        "w_qkv1": L1_attn_w_attn, "w_p1": L1_attn_w_proj,
        "gate_w": L1_ffn_gate_w, "gate_b": np.asarray(L1_ffn_gate_b)[None, :],
        "w1": L1_ffn_w1, "b1": np.asarray(L1_ffn_b1).reshape(1, -1),
        "w2": L1_ffn_w2, "b2": np.asarray(L1_ffn_b2).T,
    }
    arrays = {n: np.ascontiguousarray(a) for n, a in arrays.items()}
    nc = bacc.Bacc("TRN2", target_bir_lowering=False, num_devices=1)
    args = [nc.dram_tensor(n, a.shape, mybir.dt.from_np(a.dtype), kind="ExternalInput").ap()
            for n, a in arrays.items()]
    out = nc.dram_tensor("out", (B, P, NT, C), F32, kind="ExternalOutput").ap()
    build(nc, *args, out)
    r = run(nc, [arrays], core_ids=[0])
    got = np.asarray(r.results[0]["out"])
    return np.ascontiguousarray(got.transpose(0, 2, 1, 3)).reshape(B, HS, WS, C)
```

```python
from contextlib import ExitStack

import concourse.bass as bass
from concourse import mybir

F32 = mybir.dt.float32
F32R = mybir.dt.float32r
BF16 = mybir.dt.bfloat16
ALU = mybir.AluOpType
ACT = mybir.ActivationFunctionType
AX = mybir.AxisListType.X

B, HS, WS, C = 8, 32, 32, 96
T = HS * WS
NH, HD = 6, 16
P = 128
NT = T // P
HALF = 512
NC = T // HALF
PAIRS = NH // 2
NE, HID = 4, 384
HJ = HID // P
GROUP = C // 32
SCALE = HD ** -0.5
BIG = 1.0e30
WIN = 2 * HS - 1
GN_EPS, LN_EPS, GATE_EPS = 1e-5, 1e-5, 1e-9
REL_STEP = 4
REL_FILLS = HS // REL_STEP
ATT_FILLS = NH * NT

Q_SLOTS = (0, 0, 1, 1, 0, 2)
K_SLOTS = (0, 1, 0, 1, 2, 0)

C_ID, C_GRP, C_TIE, C_S1, C_S2, C_END = 0, 128, 224, 240, 241, 242

STAGES = ("attn0", "proj0", "qkv1", "attn1", "gn", "qkv0", "proj1", "mix")
PREFETCH = ("gn", "qkv0")
LEAD = 8


def max_cols(layer, t, kc):
    return max(0, min(HALF, (t + 1) * P - kc * HALF)) if layer else HALF


FIRST_PAIR = (1, 0)
MAX_STEPS = [[(h, t, kc) for h in range(2 * FIRST_PAIR[l], NH) for t in range(NT) for kc in range(NC)
              if max_cols(l, t, kc)] for l in (0, 1)]
PER_PAIR = [len(m) // (PAIRS - f) for m, f in zip(MAX_STEPS, FIRST_PAIR)]


def mix_steps(kind):
    ups, next_entry = kind != "first", kind != "last"
    extra = [("rel", g) for g in range(REL_FILLS)] + [("max", i) for i in range(2 * NT)]
    extra = extra if next_entry else []
    if not ups:
        return extra
    n_up, steps = NE * HJ, []
    for n in range(n_up + 1):
        here = extra[len(extra) * n // (n_up + 1):len(extra) * (n + 1) // (n_up + 1)]
        if n < n_up:
            steps.append(("up", n))
        steps += here[:1]
        if n >= 1:
            steps.append(("down", n - 1))
            if n >= 2 and (n - 1) % HJ == 0:
                steps.append(("back", n // HJ - 1))
        steps += here[1:]
    return steps + [("back", NE - 1)]


def t_fills(kind):
    return [x for x in mix_steps(kind) if x[0] in ("up", "rel", "max")]


_ATT = {"attn0": 1, "attn1": 1}
_PROJ = {"proj0": 1, "proj1": 1}
INCS = {
    "xt_in": {"gn": 16}, "x0_in": {"gn": 16}, "out_done": {"ffn": 16},
    "gstat": {"gn": 1}, "xnt_gn": {"gn": 1},
    "var_ready": {"gn": 1, **_PROJ}, "ln_var": {"gn": 1, **_PROJ}, "rs0": {"gn": 1, **_PROJ},
    "t_full": {"qkv0": 4, "attn0": ATT_FILLS, "proj0": 2, "qkv1": 4, "attn1": ATT_FILLS, "proj1": 2,
               "ffn": NE * HJ, "next": REL_FILLS + 2 * NT},
    "s_full": {"attn0": len(MAX_STEPS[0]), "attn1": len(MAX_STEPS[1]), "ffn": 2 * NE},
    "m_full": {"gn": 1, "attn0": PAIRS, "attn1": PAIRS, "ffn": 1},
    "y_full": {"ffn": NE},
    "o_free": {s: PAIRS for s in _ATT},
    "lvl1": {"qkv0": 2, "qkv1": 2}, "lvl2": {"qkv0": 2, "qkv1": 2}, "lvl3": {"qkv0": 2, "qkv1": 2},
    "wide3": {"qkv0": 2},
    "spill_q": {"qkv0": 32, "qkv1": 16}, "spill_k": {"qkv0": 32, "qkv1": 16},
    "qr_in": {"qkv0": 96}, "ab_in": {"qkv0": 192}, "l1_in": {"qkv1": 192},
    "rel_lead": {"next": REL_FILLS},
    "rowmax": {"attn0": PAIRS - 1, "attn1": PAIRS},
    "negmax_in": {s: 16 * PAIRS for s in _ATT},
    "p_used": {s: ATT_FILLS for s in _ATT},
    "h_used": {"ffn": NE * (HJ - 1)},
    "au_in": {s: 128 * PAIRS for s in _ATT},
    "lnl": _PROJ, "il0": _PROJ, "att_ready": _PROJ, "xn_tok_ready": _PROJ,
    "gate_max_ready": {"ffn": 1}, "gate_exp_ready": {"ffn": 1},
    "dve_chain": {"gn": 8, "proj0": 10, "proj1": 10, "ffn": 12},
}
for _r in "tsmy":
    INCS[f"{_r}_free"] = dict(INCS[f"{_r}_full"])
INCS["h_free"] = {"ffn": INCS["t_free"].pop("ffn")}
START = 2


def kind_of(it):
    return "first" if it is None else "last" if isinstance(it, int) else "body"


def incs(sem, stage, kind):
    table = INCS[sem]
    if stage == "mix":
        return (table.get("ffn", 0) if kind != "first" else 0) + (table.get("next", 0) if kind != "last" else 0)
    if kind == ("first", "last")[stage in PREFETCH]:
        return 0
    return table.get(stage, 0)


def before(sem, stage, kind):
    return sum(incs(sem, s, kind) for s in STAGES[:STAGES.index(stage)])


FIRST = {s: before(s, "mix", "first") + incs(s, "mix", "first") for s in INCS}
PER = {s: before(s, "mix", "body") + incs(s, "mix", "body") for s in INCS}


def upto(sem, it, stage, n):
    here = START + before(sem, stage, kind_of(it)) + n
    return here if it is None else it * PER[sem] + (FIRST[sem] + here)


def t_slot(stage, n):
    return n % 2


def s_bank(stage, n):
    return n % 2


def q_from(layer, kt):
    return kt * P if layer else 0


def build(nc, x_tok, x_t, consts, hots, masks, w_qkv0, b_qkv0, w_p0, b_p0, rel_h, rel_w, w_qkv1, w_p1, gate_w, gate_b,
          w1, b1, w2, b2, out):
    with ExitStack() as ctx:
        def sb(name, shape, dt=F32):
            return ctx.enter_context(nc.sbuf_tensor(name, shape, dt))

        def ps(name, shape):
            return ctx.enter_context(nc.psum_tensor(name, shape, F32))

        sems = {n: ctx.enter_context(nc.semaphore(n)) for n in INCS}
        xt_in = sems["xt_in"]
        x0_in = sems["x0_in"]
        out_done = sems["out_done"]
        gstat = sems["gstat"]
        xnt_gn = sems["xnt_gn"]
        var_ready = sems["var_ready"]
        ln_var = sems["ln_var"]
        rs0 = sems["rs0"]
        t_full = sems["t_full"]
        s_full = sems["s_full"]
        m_full = sems["m_full"]
        y_full = sems["y_full"]
        o_free = sems["o_free"]
        lvl1 = sems["lvl1"]
        lvl2 = sems["lvl2"]
        lvl3 = sems["lvl3"]
        wide3 = sems["wide3"]
        spill_q = sems["spill_q"]
        spill_k = sems["spill_k"]
        qr_in = sems["qr_in"]
        ab_in = sems["ab_in"]
        l1_in = sems["l1_in"]
        rel_lead = sems["rel_lead"]
        rowmax = sems["rowmax"]
        negmax_in = sems["negmax_in"]
        p_used = sems["p_used"]
        h_free = sems["h_free"]
        h_used = sems["h_used"]
        au_in = sems["au_in"]
        lnl = sems["lnl"]
        il0 = sems["il0"]
        att_ready = sems["att_ready"]
        xn_tok_ready = sems["xn_tok_ready"]
        gate_max_ready = sems["gate_max_ready"]
        gate_exp_ready = sems["gate_exp_ready"]
        dve_chain = sems["dve_chain"]
        t_free = sems["t_free"]
        s_free = sems["s_free"]
        m_free = sems["m_free"]
        y_free = sems["y_free"]
        const_in = ctx.enter_context(nc.semaphore("const_in"))
        setup = ctx.enter_context(nc.semaphore("setup"))

        cst = sb("cst", [P, C_END])
        ident = cst[:, C_ID:C_ID + P]
        group = cst[0:C, C_GRP:C_GRP + C]
        ident_b = sb("ident_b", [P, P], BF16)
        mask_q = sb("mask_q", [P, P], BF16)
        mask_k = sb("mask_k", [P, P], BF16)
        wqkv = [sb("wqkv0", [C + 1, 3 * C]), sb("wqkv1", [C, 3 * C])]
        wp = [sb("wp0", [C + 1, C]), sb("wp1", [C, C])]
        gw = sb("gw", [C + 1, NE])
        w1s = sb("w1s", [C + 1, NE * HID])
        w2s = sb("w2s", [P, NE * HJ, C])
        b2s = sb("b2s", [C, NE])
        relf = sb("relf", [C, 2, WIN])
        relr = sb("relr", [C, 2, WIN])
        rell = sb("rell", [C, 2, WIN], BF16)
        relt = sb("relt", [C, 2, WIN], BF16)

        x0 = sb("x0", [P, NT, C])
        x1 = sb("x1", [P, NT, C])
        x2 = sb("x2", [P, NT, C])
        xn_tok = sb("xn_tok", [P, NT, C])
        xnt = sb("xnt", [C + 1, T])
        xg = sb("xg", [C + 1, T])
        split = sb("split", [C, 2, 3, T], BF16)
        resid = sb("resid", [C, T])
        qr = sb("qr", [C + 1, NH, T], BF16)
        kr = sb("kr", [C + 1, NH, T], BF16)
        qa = sb("qa", [P, NH, T], BF16)
        ka = sb("ka", [P, NH, T], BF16)
        qb = sb("qb", [C + 1, NH, T], F32R)
        kb = sb("kb", [C + 1, NH, T], F32R)
        qb_raw, kb_raw = qb[:, :, :].bitcast(F32), kb[:, :, :].bitcast(F32)
        vs = [sb(f"v{l}", [P, NT, NH, 2 * HD]) for l in (0, 1)]
        probs = sb("probs", [P, 4, T])
        wide = probs[0:C, :, :].bitcast(F32R)
        mx = [sb(f"mx{l}", [P, 2, 2 * NT, NC]) for l in (0, 1)]
        mrow = sb("mrow", [P, 2, 2 * NT])
        negm = [sb("negr", [2 * NT, 2, P], F32R), sb("negb", [2 * NT, 2, P], BF16)]
        negm_raw = [negm[0][:, :, :].bitcast(F32), negm[1]]
        ot = sb("ot", [P, PAIRS, HALF])
        au = sb("au", [C, T])
        lb = sb("lb", [C, T])
        il = sb("il", [C, T])
        att = sb("att", [C + 1, T])
        hbuf = probs
        yt = au
        gs6 = sb("gs6", [C, 2, 6])
        gsm = sb("gsm", [C, 16])
        gst = sb("gst", [C, 2])
        gm = sb("gm", [C, 8])
        st6 = sb("st6", [P, NT, 6])
        sm = sb("sm", [P, 12, NT])
        g4 = sb("g4", [P, 5, NT, NE])
        g16 = sb("g16", [P, 2, NT, NE, NE])
        gden = sb("gden", [P, 4, NT])

        psT = ps("psT", [P, 2, T])
        psS = ps("psS", [P, 2, HALF])
        psOM = ps("psOM", [P, 2, HALF])
        psO, psM = psOM[:, 0, :], psOM[:, 1, :]

        scr = nc.dram_tensor("scr", [C, 2, 3, T], BF16).ap()
        scr32 = nc.dram_tensor("scr32", [C, 4, T], F32).ap()
        scr_d = scr.rearrange("(h d) s l t -> d s l h t", d=HD)
        scr32_d = scr32.rearrange("(h d) s t -> d s h t", d=HD)

        loads = [
            (cst[:, :], consts), (resid[0:2 * HS, :], hots), (probs[:, 0, 0:2 * P], masks),
            (wqkv[0][0:C, :], w_qkv0), (wqkv[0][C:C + 1, :], b_qkv0), (wqkv[1][:, :], w_qkv1),
            (wp[0][0:C, :], w_p0), (wp[0][C:C + 1, :], b_p0), (wp[1][:, :], w_p1), (gw[0:C, :], gate_w),
            (gw[C:C + 1, :], gate_b),
            (w1s[0:C, :].rearrange("c (e h) -> c e h", e=NE), w1.rearrange("e c h -> c e h")),
            (w1s[C:C + 1, :], b1), (w2s[:, :, :], w2.rearrange("e (j p) c -> p (e j) c", p=P)), (b2s[:, :], b2),
            (relf[:, 0, :], rel_h), (relf[:, 1, :], rel_w),
        ]
        n_setup = 31

        block = ctx.enter_context(nc.Block())

        @block.sync
        def _(sp):
            for sem in sems.values():
                sp.sem_inc(sem, START)
            for dst, src in loads:
                sp.dma_start(dst, src).then_inc(const_in, 16)

            def attention(it, layer):
                st = f"attn{layer}"
                for p in range(PAIRS + 1):
                    if p < PAIRS:
                        sp.wait_ge(m_free, upto("m_free", it, st, p + 1))
                        sp.dma_start((qb_raw, qr)[layer][C:C + 1, 2 * p:2 * p + 2, :].rearrange("o h (t q) -> o (h t) q", q=P),
                                     negm_raw[layer][:, p % 2, :]).then_inc(negmax_in, 16)
                    if p >= 1:
                        sp.wait_ge(o_free, upto("o_free", it, st, p))
                        for hh in range(2):
                            for c in range(NC):
                                h, j = 2 * (p - 1) + hh, 32 * (2 * hh + c)
                                rows, cols = slice(h * HD, (h + 1) * HD), slice(c * HALF, (c + 1) * HALF)
                                sp.dma_start(au[rows, cols], ot[j:j + HD, p - 1, :]).then_inc(au_in, 16)
                                sp.dma_start(lb[rows, cols],
                                             ot[j + HD:j + 2 * HD, p - 1, :]).then_inc(au_in, 16)

            def load_x(it, x_row):
                if it is None:
                    sp.wait_ge(setup, n_setup)
                else:
                    sp.wait_ge(t_full, upto("t_full", it, "attn0", 0))
                sp.dma_start(xg[0:C, :], x_t[x_row]).then_inc(xt_in, 16)
                if it is not None:
                    sp.wait_ge(t_free, upto("t_free", it, "proj0", 1))
                sp.dma_start(x0[:, :, :], x_tok[x_row]).then_inc(x0_in, 16)

            def slots0(it):
                for s, spill in ((0, spill_q), (1, spill_k)):
                    sp.wait_ge(lvl3, upto("lvl3", it, "qkv0", s + 1))
                    sp.dma_start(scr[:, s], split[:, s]).then_inc(spill, 16)
                    sp.wait_ge(wide3, upto("wide3", it, "qkv0", s + 1))
                    sp.dma_start(scr32[:, 2 * s:2 * s + 2], probs[0:C, 2 * s:2 * s + 2, :]).then_inc(spill, 16)
                sp.wait_ge(spill_q, upto("spill_q", it, "qkv0", 32))
                for n, l in enumerate(Q_SLOTS):
                    sp.dma_start(qr[n * HD:(n + 1) * HD, :, :], scr_d[:, 0, l]).then_inc(qr_in, 16)
                for n, l in enumerate(Q_SLOTS[:4]):
                    sp.dma_start(qa[n * HD:(n + 1) * HD, :, :], scr_d[:, 0, l]).then_inc(ab_in, 16)
                for n in range(2):
                    sp.dma_start(qb_raw[64 + n * HD:64 + (n + 1) * HD, :, :], scr32_d[:, n]).then_inc(ab_in, 16)
                sp.wait_ge(spill_k, upto("spill_k", it, "qkv0", 32))
                for n, l in enumerate(K_SLOTS[:4]):
                    sp.dma_start(ka[n * HD:(n + 1) * HD, :, :], scr_d[:, 1, l]).then_inc(ab_in, 16)
                for n in range(2):
                    sp.dma_start(kb_raw[64 + n * HD:64 + (n + 1) * HD, :, :], scr32_d[:, 3 - n]).then_inc(ab_in, 16)

            def slots1(it):
                for s, spill in ((0, spill_q), (1, spill_k)):
                    sp.wait_ge(lvl3, upto("lvl3", it, "qkv1", s + 1))
                    sp.dma_start(scr[:, s], split[:, s]).then_inc(spill, 16)
                sp.wait_ge(spill_q, upto("spill_q", it, "qkv1", 16))
                for n, l in enumerate(Q_SLOTS):
                    sp.dma_start(qr[n * HD:(n + 1) * HD, :, :], scr_d[:, 0, l]).then_inc(l1_in, 16)
                sp.wait_ge(spill_k, upto("spill_k", it, "qkv1", 16))
                for n, l in enumerate(K_SLOTS):
                    sp.dma_start(kr[n * HD:(n + 1) * HD, :, :], scr_d[:, 1, l]).then_inc(l1_in, 16)

            def entry(it):
                attention(it, 0)
                slots1(it)
                if kind_of(it) == "body":
                    load_x(it, it + 1)
                attention(it, 1)
                if kind_of(it) == "body":
                    slots0(it)
                sp.wait_ge(y_free, upto("y_free", it, "mix", NE))
                sp.dma_start(out[it], x2[:, :, :]).then_inc(out_done, 16)

            load_x(None, 0)
            slots0(None)
            with sp.Fori(0, B - 1) as it:
                entry(it)
            entry(B - 1)
            sp.wait_ge(out_done, START + 16 * B)

        @block.tensor
        def _(pe):
            mm = nc.tensor.matmul

            def take_t(it, stage, n):
                pe.wait_ge(t_free, upto("t_free", it, stage, n - 1))
                return psT[:, t_slot(stage, n), :]

            def take_mixed(it, n):
                fills = t_fills(kind_of(it))
                last, ups = fills[:n - 1] if n >= 2 else [], [x for x in fills[:max(n - 1, 0)] if x[0] == "up"]
                if last and last[-1][0] == "up":
                    pe.wait_ge(h_free, upto("h_free", it, "mix", len(ups)))
                else:
                    pe.wait_ge(t_free, upto("t_free", it, "mix", len(last) - len(ups)))
                return psT[:, t_slot("mix", n), :]

            def project(it, layer):
                st, k, w, x = f"qkv{layer}", C + 1 - layer, wqkv[layer], (xg, xnt)[layer]
                for s in range(2):
                    o = take_t(it, st, s)
                    for c in range(NC):
                        last = mm(o[0:C, c * HALF:(c + 1) * HALF], w[0:k, s * C:(s + 1) * C],
                                  x[0:k, c * HALF:(c + 1) * HALF], start=True, stop=True)
                    last.then_inc(t_full, 1)
                for half in range(2):
                    o = take_t(it, st, 2 + half)
                    for i in range(4):
                        t = 4 * half + i
                        last = mm(o[:, i * C:(i + 1) * C], x[0:k, t * P:(t + 1) * P], w[0:k, 2 * C:3 * C],
                                  start=True, stop=True)
                    last.then_inc(t_full, 1)

            def bias(it, fill, g):
                o = take_mixed(it, fill)
                q_cols = qr[0:C, :, :].rearrange("c h (a b) -> c h a b", b=WS)
                for i in range(REL_STEP):
                    r = REL_STEP * g + i
                    window = slice(HS - 1 - r, 2 * HS - 1 - r)
                    mm(o[0:HS, 256 * i:256 * i + NH * WS], relt[:, 0, window], qr[0:C, :, r * WS:(r + 1) * WS],
                       start=True, stop=True)
                    last = mm(o[HS:2 * HS, 256 * i:256 * i + NH * HS], relt[:, 1, window], q_cols[:, :, :, r],
                              start=True, stop=True)
                last.then_inc(t_full, 1)

            def attention(it, layer):
                st, v = f"attn{layer}", vs[layer]

                def max_scores(fill):
                    h, t, kc = MAX_STEPS[layer][fill]
                    n = max_cols(layer, t, kc)
                    pe.wait_ge(s_free, upto("s_free", it, st, fill - 1))
                    bank = psS[:, s_bank(st, fill), :]
                    q, k, rows = ((qa, ka, P), (qr, kr, C))[layer]
                    diagonal = layer == 1 and (t + 1) * P <= (kc + 1) * HALF
                    last = mm(bank[:, 0:n], q[0:rows, h, t * P:(t + 1) * P], k[0:rows, h, kc * HALF:kc * HALF + n],
                              start=True, stop=not diagonal)
                    if diagonal:
                        last = mm(bank[:, n - P:n], ident_b[:, :], mask_q[:, :], start=False, stop=True)
                    last.then_inc(s_full, 1)

                def transpose_max(p):
                    if p < FIRST_PAIR[layer]:
                        pe.wait_ge(t_free, upto("t_free", it, "attn0", 0))
                    else:
                        pe.wait_ge(rowmax, upto("rowmax", it, st, p + 1 - FIRST_PAIR[layer]))
                    pe.wait_ge(m_free, upto("m_free", it, st, p))
                    mm(psM[0:2 * NT, 0:P], mrow[:, p % 2, :], ident, is_transpose=True, start=True,
                       stop=True).then_inc(m_full, 1)

                def scores(p, kt, hh):
                    h, q0, ks = 2 * p + hh, q_from(layer, kt), slice(kt * P, (kt + 1) * P)
                    o = take_t(it, st, (p * NT + kt) * 2 + hh)
                    for c in range(NC):
                        a, b = max(q0, c * HALF), (c + 1) * HALF
                        if a >= b:
                            continue
                        if layer == 0:
                            mm(o[:, a:b], ka[:, h, ks], qa[:, h, a:b], start=True, stop=False)
                            last = mm(o[:, a:b], kb[:, h, ks], qb[:, h, a:b], start=False, stop=True)
                        else:
                            last = mm(o[:, a:b], kr[:, h, ks], qr[:, h, a:b], start=True, stop=a != q0)
                            if a == q0:
                                last = mm(o[:, a:a + P], ident_b[:, :], mask_k[:, :], start=False, stop=True)
                    last.then_inc(t_full, 1)

                def values(p, kt):
                    q0 = q_from(layer, kt)
                    if kt == 0:
                        pe.wait_ge(o_free, upto("o_free", it, st, p))
                    for hh in range(2):
                        pe.wait_ge(t_free, upto("t_free", it, st, (p * NT + kt) * 2 + hh + 1))
                        for c in range(NC):
                            a, j = max(q0, c * HALF), 32 * (2 * hh + c)
                            if a >= (c + 1) * HALF:
                                continue
                            end = NT if layer == 0 else (c + 1) * HALF // P
                            last = mm(psO[j:j + 2 * HD, a - c * HALF:HALF], v[:, kt, 2 * p + hh, :],
                                      probs[:, (2 * kt + hh) % 4, a:(c + 1) * HALF], start=kt == 0, stop=kt == end - 1)
                        last.then_inc(p_used, 1)

                n, first = PER_PAIR[layer], FIRST_PAIR[layer]
                if layer == 0:
                    pe.wait_ge(y_free, upto("y_free", it, "attn0", 0))
                else:
                    for fill in range(n):
                        max_scores(fill)
                transpose_max(0)
                for fill in range((1 - first) * n, (1 - first) * n + LEAD):
                    max_scores(fill)
                for p in range(PAIRS):
                    ahead = range((p + 1 - first) * n + (LEAD if p == 0 else 0),
                                  (p + 2 - first) * n) if p + 1 < PAIRS else ()
                    cut = [min(len(ahead), len(ahead) * i // (2 * NT - 4)) for i in range(2 * NT + 1)]
                    pe.wait_ge(negmax_in, upto("negmax_in", it, st, 16 * (p + 1)))
                    for kt in range(NT):
                        for hh in range(2):
                            scores(p, kt, hh)
                            if hh == 1 and kt >= 1:
                                values(p, kt - 1)
                            for fill in ahead[cut[2 * kt + hh]:cut[2 * kt + hh + 1]]:
                                max_scores(fill)
                        if kt == NT - 2 and p + 1 < PAIRS:
                            transpose_max(p + 1)
                    values(p, NT - 1)

            def out_project(it, layer):
                st, k = f"proj{layer}", C + 1 - layer
                pe.wait_ge(att_ready, upto("att_ready", it, st, 1))
                o = take_t(it, st, 0)
                for t in range(NT):
                    a = (t // 4) * HALF + (t % 4) * C
                    last = mm(o[:, a:a + C], att[0:k, t * P:(t + 1) * P], wp[layer][0:k, :], start=True, stop=True)
                last.then_inc(t_full, 1)
                pe.wait_ge(xn_tok_ready, upto("xn_tok_ready", it, st, 1))
                o = take_t(it, st, 1)
                for t in range(NT):
                    last = mm(o[0:C, t * P:(t + 1) * P], xn_tok[:, t, :], ident, is_transpose=True, start=True,
                              stop=True)
                last.then_inc(t_full, 1)

            def gate_scores(it):
                pe.wait_ge(m_free, upto("m_free", it, "mix", 0))
                for t in range(NT):
                    last = mm(psM[:, t * NE:(t + 1) * NE], xnt[:, t * P:(t + 1) * P], gw[:, :], start=True, stop=True)
                last.then_inc(m_full, 1)

            def up(it, fill, n):
                o, (x, j) = take_mixed(it, fill), divmod(n, HJ)
                a = x * HID + j * P
                for c in range(NC):
                    last = mm(o[:, c * HALF:(c + 1) * HALF], w1s[:, a:a + P], xnt[:, c * HALF:(c + 1) * HALF],
                              start=True, stop=True)
                last.then_inc(t_full, 1)

            def down(it, n):
                x, j = divmod(n, HJ)
                if j == 0:
                    pe.wait_ge(s_free, upto("s_free", it, "mix", 2 * x))
                pe.wait_ge(h_free, upto("h_free", it, "mix", n + 1))
                for c in range(NC):
                    last = mm(psS[0:C, c, :], w2s[:, n, :], hbuf[:, n % 4, c * HALF:(c + 1) * HALF], start=j == 0,
                              stop=j == HJ - 1)
                    if j == HJ - 1:
                        last.then_inc(s_full, 1)
                    elif c == NC - 1:
                        last.then_inc(h_used, 1)

            def back(it, x):
                pe.wait_ge(s_free, upto("s_free", it, "mix", 2 * x + 2))
                pe.wait_ge(y_free, upto("y_free", it, "mix", x))
                if x == 0:
                    pe.wait_ge(m_free, upto("m_free", it, "mix", 1))
                    pe.wait_ge(o_free, upto("o_free", it, "mix", 0))
                for t in range(NT):
                    last = mm(psOM[:, t // 4, (t % 4) * C:(t % 4 + 1) * C], yt[:, t * P:(t + 1) * P],
                              ident[0:C, 0:C], is_transpose=True, start=True, stop=True)
                last.then_inc(y_full, 1)

            def first_maxima(it, fill, i):
                o, (h, t) = take_mixed(it, fill), divmod(i, NT)
                for c in range(NC):
                    last = mm(o[:, c * HALF:(c + 1) * HALF], qa[:, h, t * P:(t + 1) * P],
                              ka[:, h, c * HALF:(c + 1) * HALF], start=True, stop=True)
                last.then_inc(t_full, 1)

            def mix(it):
                fills = t_fills(kind_of(it))
                if it is not None:
                    pe.wait_ge(t_free, upto("t_free", it, "proj1", 2))
                    gate_scores(it)
                for what, n in mix_steps(kind_of(it)):
                    if what == "up":
                        up(it, fills.index((what, n)), n)
                    elif what == "down":
                        down(it, n)
                    elif what == "back":
                        back(it, n)
                    elif what == "rel":
                        pe.wait_ge(qr_in, upto("qr_in", it, "mix", 0))
                        bias(it, fills.index((what, n)), n)
                    else:
                        if n == 0:
                            pe.wait_ge(ab_in, upto("ab_in", it, "mix", 0))
                            pe.wait_ge(t_free, upto("t_free", it, "mix", REL_FILLS))
                        first_maxima(it, fills.index((what, n)), n)

            def next_qkv(it):
                pe.wait_ge(gstat, upto("gstat", it, "gn", 1))
                pe.wait_ge(m_free, upto("m_free", it, "gn", 0))
                mm(psM[0:C, 0:2], group, gst[:, :], start=True, stop=True).then_inc(m_full, 1)
                pe.wait_ge(xnt_gn, upto("xnt_gn", it, "gn", 1))
                project(it, 0)

            def entry(it):
                attention(it, 0)
                out_project(it, 0)
                pe.wait_ge(t_free, upto("t_free", it, "proj0", 2))
                project(it, 1)
                pe.wait_ge(l1_in, upto("l1_in", it, "qkv1", 192))
                pe.wait_ge(t_free, upto("t_free", it, "qkv1", 4))
                attention(it, 1)
                if kind_of(it) == "body":
                    next_qkv(it)
                out_project(it, 1)
                mix(it)

            pe.wait_ge(const_in, 16 * len(loads))
            pe.wait_ge(setup, n_setup)
            next_qkv(None)
            mix(None)
            with pe.Fori(0, B - 1) as it:
                entry(it)
            entry(B - 1)

        def rel_views(dst, base, g, o):
            o = o.rearrange("p (i r) -> p i r", r=256)[:, :, 0:NH * HS]
            r = slice(REL_STEP * g, REL_STEP * (g + 1))
            return ((dst[base:base + HS].rearrange("p h (a b) -> p a h b", b=WS)[:, r],
                     o[0:HS].rearrange("p i (h b) -> p i h b", h=NH)),
                    (dst[base + HS:base + 2 * HS].rearrange("p h (a b) -> p h a b", b=WS)[:, :, :, r],
                     o[HS:2 * HS].rearrange("p i (h a) -> p h a i", h=NH)))

        @block.scalar
        def _(act):
            A = nc.scalar.activation

            def rstd_guess(it, stage, v, lnv, y):
                act.wait_ge(var_ready, upto("var_ready", it, stage, 1))
                A(lnv, v, ACT.Ln).then_inc(ln_var, 1)
                act.wait_ge(ln_var, upto("ln_var", it, stage, 1))
                A(y, lnv, ACT.Exp, scale=-0.5).then_inc(rs0, 1)

            def split_levels(it, layer):
                st = f"qkv{layer}"
                act.wait_ge(spill_q, upto("spill_q", it, st, 0))
                act.wait_ge(spill_k, upto("spill_k", it, st, 0))
                for s in range(2):
                    act.wait_ge(t_full, upto("t_full", it, st, s + 1))
                    A(split[:, s, 0, :], psT[0:C, t_slot(st, s), :], ACT.Copy,
                      scale=(1.0, SCALE)[s]).then_inc(lvl1, 1)
                for s in range(2):
                    act.wait_ge(t_free, upto("t_free", it, st, s + 1))
                    A(split[:, s, 1, :], resid[:, :], ACT.Copy).then_inc(lvl2, 1)
                    if layer == 0:
                        act.wait_ge(lvl1, upto("lvl1", it, st, s + 1))
                        A(wide[:, 2 * s, :], split[:, s, 0, :], ACT.Copy)
                for b in range(2):
                    act.wait_ge(t_full, upto("t_full", it, st, 3 + b))
                    A(vs[layer][:, 4 * b:4 * b + 4, :, 0:HD],
                      psT[:, t_slot(st, 2 + b), 0:4 * C].rearrange("p (t h d) -> p t h d", t=4, h=NH),
                      ACT.Copy).then_inc(t_free, 1)
                if layer == 0:
                    for s in range(2):
                        act.wait_ge(lvl3, upto("lvl3", it, st, s + 1))
                        A(wide[:, 2 * s + 1, :], split[:, s, 2, :], ACT.Copy).then_inc(wide3, 1)

            def attention(it, layer):
                st = f"attn{layer}"

                def neg_max(p):
                    act.wait_ge(m_full, upto("m_full", it, st, p + 1))
                    act.wait_ge(negmax_in, upto("negmax_in", it, st, 16 * max(p - 1, 0)))
                    A(negm[layer][:, p % 2, :], psM[0:2 * NT, 0:P], ACT.Copy, scale=-1.0).then_inc(m_free, 1)

                def evacuate(p):
                    act.wait_ge(p_used, upto("p_used", it, st, 2 * NT * (p + 1)))
                    act.wait_ge(au_in, upto("au_in", it, st, 0))
                    A(ot[:, p, :], psO, ACT.Copy).then_inc(o_free, 1)

                neg_max(0)
                for p in range(PAIRS):
                    for kt in range(NT):
                        for hh in range(2):
                            n = (p * NT + kt) * 2 + hh
                            act.wait_ge(t_full, upto("t_full", it, st, n + 1))
                            act.wait_ge(p_used, upto("p_used", it, st, max(n - 3, 0)))
                            q0 = q_from(layer, kt)
                            A(probs[:, n % 4, q0:T], psT[:, t_slot(st, n), q0:T], ACT.Exp).then_inc(t_free, 1)
                        if kt == 0 and p >= 1:
                            evacuate(p - 1)
                        if kt == NT - 2 and p + 1 < PAIRS:
                            neg_max(p + 1)
                if layer == 1 and kind_of(it) == "body":
                    rstd_guess(it, "gn", gm[:, 3:4], gm[:, 4:5], gm[:, 5:6])
                evacuate(PAIRS - 1)

            def normalise(it, layer):
                st = f"proj{layer}"
                act.wait_ge(au_in, upto("au_in", it, f"attn{layer}", 128 * PAIRS))
                A(il[:, :], lb[:, :], ACT.Ln).then_inc(lnl, 1)
                act.wait_ge(lnl, upto("lnl", it, st, 1))
                A(il[:, :], il[:, :], ACT.Exp, scale=-1.0).then_inc(il0, 1)
                rstd_guess(it, st, sm[:, 5, :], sm[:, 6, :], sm[:, 7, :])
                act.wait_ge(t_full, upto("t_full", it, st, 2))
                A(xnt[0:C, :], psT[0:C, t_slot(st, 1), :], ACT.Copy).then_inc(t_free, 1)

            def mix(it):
                fills = t_fills(kind_of(it))
                if it is not None:
                    act.wait_ge(gate_max_ready, upto("gate_max_ready", it, "mix", 1))
                    A(g4[:, 1], g4[:, 0], ACT.Exp).then_inc(gate_exp_ready, 1)
                    act.wait_ge(spill_q, upto("spill_q", it, "mix", 0))
                    act.wait_ge(spill_k, upto("spill_k", it, "mix", 0))
                for fill, (what, n) in enumerate(fills):
                    if what == "up":
                        used = n - 4
                        if used >= 0 and used % HJ == HJ - 1:
                            act.wait_ge(s_full, upto("s_full", it, "mix", 2 * (used // HJ + 1)))
                        elif used >= 0:
                            act.wait_ge(h_used, upto("h_used", it, "mix", (HJ - 1) * (used // HJ) + used % HJ + 1))
                        act.wait_ge(t_full, upto("t_full", it, "mix", fill + 1))
                        A(hbuf[:, n % 4, :], psT[:, t_slot("mix", fill), :], ACT.Gelu).then_inc(h_free, 1)
                    elif what == "rel":
                        act.wait_ge(t_full, upto("t_full", it, "mix", fill + 1))
                        rows, cols = rel_views(qa, 64, n, psT[:, t_slot("mix", fill), :])
                        A(rows[0], rows[1], ACT.Copy)
                        A(cols[0], cols[1], ACT.Copy).then_inc(rel_lead, 1)

            def entry(it):
                attention(it, 0)
                normalise(it, 0)
                split_levels(it, 1)
                attention(it, 1)
                if kind_of(it) == "body":
                    split_levels(it, 0)
                normalise(it, 1)
                mix(it)

            act.wait_ge(const_in, 16 * len(loads))
            act.wait_ge(setup, n_setup)
            rstd_guess(None, "gn", gm[:, 3:4], gm[:, 4:5], gm[:, 5:6])
            split_levels(None, 0)
            mix(None)
            with act.Fori(0, B - 1) as it:
                entry(it)
            entry(B - 1)

        @block.vector
        def _(dve):
            V = nc.vector
            done = [0]

            def ready(ins):
                done[0] += 1
                ins.then_inc(setup, 1)
                dve.wait_ge(setup, done[0])

            dve.wait_ge(const_in, 16 * len(loads))
            hot = resid[0:2 * HS, :]
            ready(V.tensor_copy(ident_b[:, :], ident))
            ready(V.tensor_copy(mask_q[:, :], probs[:, 0, 0:P]))
            ready(V.tensor_copy(mask_k[:, :], probs[:, 0, P:2 * P]))
            for h in range(NH):
                ready(V.tensor_copy(ka[64:128, h, :], hot))
                ready(V.tensor_copy(kb[0:64, h, :], hot))
            for ones in (kr[C:C + 1, :, :], kb[C:C + 1, :, :].bitcast(F32), xnt[C:C + 1, :],
                         xg[C:C + 1, :], att[C:C + 1, :],
                         vs[0][:, :, :, HD:2 * HD], vs[1][:, :, :, HD:2 * HD]):
                ready(V.memset(ones, 1.0))
            ready(V.memset(mx[0][:, :, :, :], -BIG))
            ready(V.memset(mx[1][:, :, :, :], -BIG))
            ready(V.tensor_copy(rell[:, :, :], relf[:, :, :]))
            ready(V.scalar_tensor_tensor(out=relr[:, :, :], in0=rell[:, :, :], scalar=cst[0:C, C_S1:C_S1 + 1],
                                         in1=relf[:, :, :], op0=ALU.mult, op1=ALU.add))
            ready(V.tensor_copy(rell[:, :, :], relr[:, :, :]))
            ready(V.scalar_tensor_tensor(out=relt[:, :, :], in0=rell[:, :, :], scalar=cst[0:C, C_S2:C_S2 + 1],
                                         in1=relr[:, :, :], op0=ALU.mult, op1=ALU.add))
            while done[0] < n_setup:
                ready(V.memset(gden[:, 3, :], 1.0))
            assert done[0] == n_setup, done[0]

            count = {}

            def link(it, stage, ins):
                key = (kind_of(it), stage)
                count[key] = count.get(key, 0) + 1
                ins.then_inc(dve_chain, 1)
                dve.wait_ge(dve_chain, upto("dve_chain", it, stage, count[key]))

            def newton(it, stage, v, y, tmp, out):
                dve.wait_ge(rs0, upto("rs0", it, stage, 1))
                link(it, stage, V.tensor_tensor(tmp, y, y, ALU.mult))
                link(it, stage, V.tensor_tensor(tmp, tmp, v, ALU.mult))
                link(it, stage, V.tensor_scalar(tmp, tmp, -0.5, 1.5, ALU.mult, ALU.add))
                link(it, stage, V.tensor_tensor(out, y, tmp, ALU.mult))

            def group_norm(it):
                st = "gn"
                dve.wait_ge(xt_in, upto("xt_in", it, st, 16))
                for c in range(NC):
                    ins = V.bn_stats(gs6[:, c, :], xg[0:C, c * HALF:(c + 1) * HALF])
                link(it, st, ins)
                means = gs6[:, :, :].rearrange("p c (k s) -> p (c k) s", s=3)[:, :, 1]
                sqs = gs6[:, :, :].rearrange("p c (k s) -> p (c k) s", s=3)[:, :, 2]
                link(it, st, V.tensor_tensor(gsm[:, 0:4], means, means, ALU.mult))
                V.reduce_sum(gst[:, 0:1], means, AX)
                V.reduce_sum(gsm[:, 4:5], gsm[:, 0:4], AX)
                link(it, st, V.reduce_sum(gsm[:, 5:6], sqs, AX))
                V.scalar_tensor_tensor(out=gst[:, 1:2], in0=gsm[:, 5:6], scalar=4.0 / T, in1=gsm[:, 4:5],
                                       op0=ALU.mult, op1=ALU.add).then_inc(gstat, 1)
                dve.wait_ge(m_full, upto("m_full", it, st, 1))
                V.tensor_scalar(gm[:, 0:2], psM[0:C, 0:2], 0.25, None, ALU.mult).then_inc(m_free, 1)
                dve.wait_ge(m_free, upto("m_free", it, st, 1))
                link(it, st, V.scalar_tensor_tensor(out=gm[:, 2:3], in0=gm[:, 0:1], scalar=gm[:, 0:1], in1=gm[:, 1:2],
                                                op0=ALU.mult, op1=ALU.subtract))
                V.tensor_scalar(gm[:, 3:4], gm[:, 2:3], -1.0, GN_EPS, ALU.mult, ALU.add).then_inc(var_ready, 1)
                newton(it, st, gm[:, 3:4], gm[:, 5:6], gm[:, 6:7], gm[:, 7:8])
                V.tensor_scalar(xg[0:C, :], xg[0:C, :], gm[:, 0:1], gm[:, 7:8], ALU.subtract,
                                ALU.mult).then_inc(xnt_gn, 1)

            def residuals(it, layer):
                st = f"qkv{layer}"
                for s in range(2):
                    dve.wait_ge(lvl1, upto("lvl1", it, st, s + 1))
                    if s == 1:
                        dve.wait_ge(lvl3, upto("lvl3", it, st, 1))
                    V.scalar_tensor_tensor(out=resid[:, :], in0=psT[0:C, t_slot(st, s), :],
                                           scalar=(1.0, SCALE)[s], in1=split[:, s, 0, :], op0=ALU.mult,
                                           op1=ALU.subtract).then_inc(t_free, 1)
                    dve.wait_ge(lvl2, upto("lvl2", it, st, s + 1))
                    V.tensor_tensor(split[:, s, 2, :], resid[:, :], split[:, s, 1, :],
                                    ALU.subtract).then_inc(lvl3, 1)

            def maxima(it, layer):
                st = f"attn{layer}"
                for fill, (h, t, kc) in enumerate(MAX_STEPS[layer]):
                    dve.wait_ge(s_full, upto("s_full", it, st, fill + 1))
                    p = h // 2
                    V.reduce_max(mx[layer][:, p % 2, (h % 2) * NT + t, kc:kc + 1],
                                 psS[:, s_bank(st, fill), 0:max_cols(layer, t, kc)], AX).then_inc(s_free, 1)
                    if (fill + 1) % PER_PAIR[layer] == 0:
                        dve.wait_ge(s_free, upto("s_free", it, st, fill + 1))
                        dve.wait_ge(m_full, upto("m_full", it, st, max(p - 1, 0)))
                        V.tensor_tensor(mrow[:, p % 2, :], mx[layer][:, p % 2, :, 0], mx[layer][:, p % 2, :, 1],
                                        ALU.max).then_inc(rowmax, 1)

            def normalise(it, layer, res, new):
                st = f"proj{layer}"
                dve.wait_ge(il0, upto("il0", it, st, 1))
                link(it, st, V.tensor_tensor(lb[:, :], lb[:, :], il[:, :], ALU.mult))
                link(it, st, V.scalar_tensor_tensor(out=il[:, :], in0=lb[:, :], scalar=2.0, in1=il[:, :],
                                                op0=ALU.subtract, op1=ALU.mult))
                V.scalar_tensor_tensor(out=att[0:C, :], in0=il[:, :], scalar=-1.0, in1=au[:, :], op0=ALU.mult,
                                       op1=ALU.mult).then_inc(att_ready, 1)
                if layer == 0:
                    dve.wait_ge(x0_in, upto("x0_in", it, st, 0))
                else:
                    dve.wait_ge(out_done, upto("out_done", it, st, 0))
                dve.wait_ge(t_full, upto("t_full", it, st, 1))
                o = psT[:, t_slot(st, 0), :].rearrange("p (b r) -> p b r", b=2)[:, :, 0:4 * C]
                V.tensor_tensor(new[:, :, :].rearrange("p (b t) c -> p b (t c)", b=2), o,
                                res[:, :, :].rearrange("p (b t) c -> p b (t c)", b=2),
                                ALU.add).then_inc(t_free, 1)
                dve.wait_ge(t_free, upto("t_free", it, st, 1))
                for t in range(NT):
                    ins = V.bn_stats(st6[:, t, :], new[:, t, :])
                link(it, st, ins)
                me, ve, mo, vo = (st6[:, :, k] for k in (1, 2, 4, 5))
                V.tensor_tensor(sm[:, 0, :], me, mo, ALU.add)
                V.tensor_tensor(sm[:, 1, :], me, mo, ALU.subtract)
                link(it, st, V.tensor_tensor(sm[:, 2, :], ve, vo, ALU.add))
                V.tensor_scalar(sm[:, 8, :], sm[:, 0, :], 0.5, None, ALU.mult)
                link(it, st, V.scalar_tensor_tensor(out=sm[:, 3, :], in0=sm[:, 1, :], scalar=0.25, in1=sm[:, 1, :],
                                                op0=ALU.mult, op1=ALU.mult))
                link(it, st, V.scalar_tensor_tensor(out=sm[:, 4, :], in0=sm[:, 2, :], scalar=1.0 / C, in1=sm[:, 3, :],
                                                op0=ALU.mult, op1=ALU.add))
                V.tensor_scalar(sm[:, 5, :], sm[:, 4, :], LN_EPS, None, ALU.add).then_inc(var_ready, 1)
                newton(it, st, sm[:, 5, :], sm[:, 7, :], sm[:, 9, :], sm[:, 10, :])
                for t in range(NT):
                    ins = V.tensor_scalar(xn_tok[:, t, :], new[:, t, :], sm[:, 8, t:t + 1], sm[:, 10, t:t + 1],
                                          ALU.subtract, ALU.mult)
                ins.then_inc(xn_tok_ready, 1)

            def gates(it):
                st = "mix"
                dve.wait_ge(m_full, upto("m_full", it, st, 1))
                s = psM[:, 0:NT * NE].rearrange("p (t x) -> p t x", x=NE)

                def over(row):
                    return row.unsqueeze(2).to_broadcast([P, NT, NE])

                link(it, st, V.reduce_max(gden[:, 0, :], s, AX))
                V.tensor_tensor(g4[:, 0], s, over(gden[:, 0, :]), ALU.subtract).then_inc(gate_max_ready, 1)
                dve.wait_ge(gate_exp_ready, upto("gate_exp_ready", it, st, 1))
                link(it, st, V.reduce_sum(gden[:, 1, :], g4[:, 1], AX))
                link(it, st, V.reciprocal(gden[:, 2, :], gden[:, 1, :]))
                link(it, st, V.tensor_tensor(g4[:, 2], g4[:, 1], over(gden[:, 2, :]), ALU.mult))
                shape = [P, NT, NE, NE]
                mine = g4[:, 2].unsqueeze(3).to_broadcast(shape)
                other = g4[:, 2].unsqueeze(2).to_broadcast(shape)
                V.tensor_tensor(g16[:, 0], other, mine, ALU.is_gt)
                link(it, st, V.tensor_tensor(g16[:, 1], other, mine, ALU.is_equal))
                tie = cst[:, C_TIE:C_TIE + NE * NE].rearrange("p (i j) -> p i j", j=NE).unsqueeze(1).to_broadcast(shape)
                link(it, st, V.tensor_tensor(g16[:, 1], g16[:, 1], tie, ALU.mult))
                link(it, st, V.tensor_tensor(g16[:, 0], g16[:, 0], g16[:, 1], ALU.add))
                link(it, st, V.reduce_sum(g4[:, 3], g16[:, 0], AX))
                link(it, st, V.scalar_tensor_tensor(out=g4[:, 4], in0=g4[:, 3], scalar=1.5, in1=g4[:, 2],
                                                op0=ALU.is_lt, op1=ALU.mult))
                link(it, st, V.reduce_sum(gden[:, 0, :], g4[:, 4], AX))
                link(it, st, V.tensor_scalar(gden[:, 1, :], gden[:, 0, :], GATE_EPS, None, ALU.add))
                link(it, st, V.reciprocal(gden[:, 2, :], gden[:, 1, :]))
                V.tensor_tensor(g4[:, 0], g4[:, 4], over(gden[:, 2, :]), ALU.mult).then_inc(m_free, 1)

            def mix(it):
                st, fills = "mix", t_fills(kind_of(it))
                if it is not None:
                    gates(it)
                    dve.wait_ge(m_free, upto("m_free", it, st, 1))
                for what, n in mix_steps(kind_of(it)):
                    if what == "down" and n % HJ == HJ - 1:
                        x = n // HJ
                        dve.wait_ge(y_full, upto("y_full", it, st, x))
                        for c in range(NC):
                            dve.wait_ge(s_full, upto("s_full", it, st, 2 * x + c + 1))
                            V.tensor_scalar(yt[:, c * HALF:(c + 1) * HALF], psS[0:C, c, :], b2s[:, x:x + 1], None,
                                            ALU.add).then_inc(s_free, 1)
                    elif what == "back":
                        dve.wait_ge(y_full, upto("y_full", it, st, n + 1))
                        dve.wait_ge(y_free, upto("y_free", it, st, n))
                        for t in range(NT):
                            y = psOM[:, t // 4, (t % 4) * C:(t % 4 + 1) * C]
                            ins = V.scalar_tensor_tensor(out=x2[:, t, :], in0=y, scalar=g4[:, 0, t, n:n + 1],
                                                         in1=x2[:, t, :], op0=ALU.mult, op1=ALU.add)
                        ins.then_inc(y_free, 1)
                    elif what == "rel":
                        fill = fills.index((what, n))
                        dve.wait_ge(rel_lead, upto("rel_lead", it, st, n + 1))
                        o = psT[:, t_slot(st, fill), :]
                        for lead, rest in zip(rel_views(qa, 64, n, o), rel_views(qb, 0, n, o)):
                            ins = V.tensor_tensor(rest[0], rest[1], lead[0], ALU.subtract)
                        ins.then_inc(t_free, 1)
                    elif what == "max":
                        fill = fills.index((what, n))
                        if n == 0:
                            dve.wait_ge(m_full, upto("m_full", it, st, 0))
                        dve.wait_ge(t_full, upto("t_full", it, st, fill + 1))
                        V.reduce_max(mrow[:, 0, n:n + 1], psT[:, t_slot(st, fill), :], AX).then_inc(t_free, 1)

            def entry(it):
                maxima(it, 0)
                normalise(it, 0, x0, x1)
                residuals(it, 1)
                maxima(it, 1)
                if kind_of(it) == "body":
                    group_norm(it)
                    residuals(it, 0)
                normalise(it, 1, x1, x2)
                mix(it)

            group_norm(None)
            residuals(None, 0)
            mix(None)
            with dve.Fori(0, B - 1) as it:
                entry(it)
            entry(B - 1)
            for (kind, stage), n in count.items():
                assert incs("dve_chain", stage, kind) == n, (stage, kind, n)




def _constants(np):
    c = np.zeros((P, C_END), np.float32)
    i, j = np.arange(P)[:, None], np.arange(P)[None, :]
    c[:, C_ID:C_ID + P] = i == j
    g = np.arange(C) // GROUP
    c[0:C, C_GRP:C_GRP + C] = (g[:, None] == g[None, :]) / GROUP
    x = np.arange(NE)
    c[:, C_TIE:C_TIE + NE * NE] = (x[None, :] < x[:, None]).reshape(1, -1)
    level = np.repeat(K_SLOTS, HD)
    c[0:C, C_S1] = np.where(level >= 1, -1, 0)
    c[0:C, C_S2] = np.where(level >= 2, -1, 0)
    return c


def _hots(np):
    key = np.arange(T)
    return np.concatenate([key[None, :] // WS == np.arange(HS)[:, None],
                           key[None, :] % WS == np.arange(WS)[:, None]]).astype(np.float32)


def _masks(np):
    i, j = np.arange(P)[:, None], np.arange(P)[None, :]
    return np.concatenate([np.where(j > i, -BIG, 0), np.where(i > j, -BIG, 0)], 1).astype(np.float32)


def kernel(x, L0_conv_qkv_w, L0_conv_qkv_b, L0_conv_proj_w, L0_conv_proj_b, L0_conv_rel_pos_h, L0_conv_rel_pos_w,
           L1_attn_w_attn, L1_attn_w_proj, L1_ffn_gate_w, L1_ffn_gate_b, L1_ffn_w1, L1_ffn_b1, L1_ffn_w2, L1_ffn_b2):
    import numpy as np
    import concourse.bacc as bacc
    from concourse.bass_utils import run_bass_kernel_spmd as run

    def table(r):
        return np.tile(np.asarray(r)[::-1].T, (len(K_SLOTS), 1))

    x = np.asarray(x)
    arrays = {
        "x_tok": x.reshape(B, NT, P, C).transpose(0, 2, 1, 3),
        "x_t": x.reshape(B, T, C).transpose(0, 2, 1),
        "consts": _constants(np), "hots": _hots(np), "masks": _masks(np),
        "w_qkv0": L0_conv_qkv_w, "b_qkv0": np.asarray(L0_conv_qkv_b)[None, :],
        "w_p0": L0_conv_proj_w, "b_p0": np.asarray(L0_conv_proj_b)[None, :],
        "rel_h": table(L0_conv_rel_pos_h), "rel_w": table(L0_conv_rel_pos_w),
        "w_qkv1": L1_attn_w_attn, "w_p1": L1_attn_w_proj,
        "gate_w": L1_ffn_gate_w, "gate_b": np.asarray(L1_ffn_gate_b)[None, :],
        "w1": L1_ffn_w1, "b1": np.asarray(L1_ffn_b1).reshape(1, -1),
        "w2": L1_ffn_w2, "b2": np.asarray(L1_ffn_b2).T,
    }
    arrays = {n: np.ascontiguousarray(a) for n, a in arrays.items()}
    nc = bacc.Bacc("TRN2", target_bir_lowering=False, num_devices=1)
    args = [nc.dram_tensor(n, a.shape, mybir.dt.from_np(a.dtype), kind="ExternalInput").ap()
            for n, a in arrays.items()]
    out = nc.dram_tensor("out", (B, P, NT, C), F32, kind="ExternalOutput").ap()
    build(nc, *args, out)
    r = run(nc, [arrays], core_ids=[0])
    got = np.asarray(r.results[0]["out"])
    return np.ascontiguousarray(got.transpose(0, 2, 1, 3)).reshape(B, HS, WS, C)
```

```python
from contextlib import ExitStack

import concourse.bass as bass
from concourse import mybir

F32 = mybir.dt.float32
F32R = mybir.dt.float32r
BF16 = mybir.dt.bfloat16
ALU = mybir.AluOpType
ACT = mybir.ActivationFunctionType
AX = mybir.AxisListType.X

B, HS, WS, C = 8, 32, 32, 96
T = HS * WS
NH, HD = 6, 16
P = 128
NT = T // P
HALF = 512
NC = T // HALF
PAIRS = NH // 2
NE, HID = 4, 384
HJ = HID // P
GROUP = C // 32
SCALE = HD ** -0.5
BIG = 1.0e30
WIN = 2 * HS - 1
GN_EPS, LN_EPS, GATE_EPS = 1e-5, 1e-5, 1e-9
REL_STEP = 4
REL_FILLS = HS // REL_STEP
ATT_FILLS = NH * NT

Q_SLOTS = (0, 0, 1, 1, 0, 2)
K_SLOTS = (0, 1, 0, 1, 2, 0)

C_ID, C_GRP, C_TIE, C_S1, C_S2, C_END = 0, 128, 224, 240, 241, 242

STAGES = ("gn", "attn1", "qkv0", "attn1b", "turn", "attn0", "norm", "mix")
OWN = ("attn1", "attn1b", "norm")
NA = 3
NB = NE - NA
LEAD = 8


def max_cols(layer, t, kc):
    return max(0, min(HALF, (t + 1) * P - kc * HALF)) if layer else HALF


MAX_STEPS = [[(h, t, kc) for h in range(2, NH) for t in range(NT) for kc in range(NC) if max_cols(l, t, kc)]
             for l in (0, 1)]
PER_PAIR = [len(m) // (PAIRS - 1) for m in MAX_STEPS]
MAXES = [("max", i) for i in range(2 * NT)]


RELS = [("rel", g) for g in range(REL_FILLS)]
TURN = ([("up", 9), ("up", 10)] + RELS[:2] + [("down", 9)] + RELS[2:4] + [("down", 10)] + RELS[4:]
        + [("up", 11), ("ln", 1)] + MAXES[:2] + [("down", 11)] + MAXES[2:6] + [("back", 3)] + MAXES[6:])
MIX = [("up", 0), ("up", 1), ("down", 0), ("up", 2), ("down", 1), ("ln", 0), ("up", 3), ("down", 2), ("den", 0),
       ("up", 4), ("down", 3), ("res", 0), ("back", 0), ("up", 5), ("down", 4), ("nrm", 0), ("up", 6), ("down", 5),
       ("tr", 0), ("up", 7), ("qk", 0), ("qk", 1), ("down", 6), ("val", 0), ("lev", 0), ("val", 1), ("back", 1),
       ("up", 8), ("down", 7), ("down", 8), ("back", 2),
       ("up", 9), ("up", 10), ("down", 9), ("up", 11), ("down", 10), ("down", 11), ("back", 3)] + MAXES


def parts(stage, kind):
    last, first = kind == "last", kind == "first"
    if stage == "turn":
        return [p for p, there in (("b", kind in ("body", "last")), ("own_turn", not first), ("next_turn", not last))
                if there]
    return [p for p, there in (("a", not first), ("b", last), ("next_mix", not last)) if there]


def part_of(stage, what):
    if what[0] in ("up", "down", "back"):
        return "a" if (what[1] if what[0] == "back" else what[1] // HJ) < NA else "b"
    return "own_turn" if what == ("ln", 1) else "next_" + stage


def steps(stage, kind):
    return [x for x in (TURN if stage == "turn" else MIX) if part_of(stage, x) in parts(stage, kind)]


def fills(stage, kind):
    return [x for x in steps(stage, kind) if x[0] in ("up", "rel", "max", "res", "tr", "qk", "val")]


def by_act(what):
    return what[0] in ("up", "tr", "val")


_ATT = {"attn0": 1, "attn1": 1}
_PROJ = {"norm": 1, "next_mix": 1}
_DEN = {"own_turn": 1, "next_mix": 1}
_LEVELS = {"qkv0": 2, "next_mix": 2}
_NORMS = {"gn": 1, **_PROJ}
INCS = {
    "xt_in": {"next_mix": 16}, "x0_in": {"attn0": 16}, "out_done": {"b": 16},
    "gstat": {"gn": 1}, "xnt_gn": {"gn": 1},
    "var_ready": _NORMS, "ln_var": _NORMS, "rs0": _NORMS,
    "t_full": {"qkv0": 4, "attn0": ATT_FILLS, "attn1": 2 * NT, "attn1b": ATT_FILLS - 2 * NT,
               "next_turn": REL_FILLS + 2 * NT, "a": NA * HJ, "b": NB * HJ, "next_mix": 6 + 2 * NT},
    "s_full": {"attn0": len(MAX_STEPS[0]), "attn1": len(MAX_STEPS[1]), "norm": 4, "a": 2 * NA,
               "b": 2 * NB},
    "m_full": {"attn0": PAIRS, "attn1": 2, "attn1b": PAIRS - 2, "a": 1},
    "gsum_full": {"gn": 1}, "gsum_free": {"gn": 1},
    "y_full": {"a": NA, "b": NB},
    "o_free": {s: PAIRS for s in _ATT},
    "lvl1": _LEVELS, "lvl2": _LEVELS, "lvl3": {"qkv0": 2, "next_mix": 1},
    "lvl3_k1": {"next_mix": 1}, "wide3": {"qkv0": 2},
    "spill_q": {"qkv0": 32, "next_mix": 16}, "spill_k": {"qkv0": 32, "next_mix": 16},
    "qr_in": {"qkv0": 192}, "ab_in": {"qkv0": 192}, "l1_in": {"next_mix": 192}, "l1_first": {"next_mix": 192},
    "rel_lead": {"next_turn": 2 * REL_FILLS},
    "rowmax": {s: PAIRS - 1 for s in _ATT},
    "negmax_in": {s: 16 * PAIRS for s in _ATT},
    "p_used": {s: ATT_FILLS for s in _ATT},
    "h_used": {"a": NA * (HJ - 1), "b": NB * (HJ - 1)},
    "au_in": {s: 128 * PAIRS for s in _ATT},
    "lnl": _DEN, "il0": _DEN, "att_ready": _DEN, "xn_tok_ready": _PROJ,
    "gate_max_ready": {"a": 1}, "gate_exp_ready": {"a": 1},
    "pool_chain": {"own_turn": 4},
    "dve_chain": {"gn": 8, "norm": 8, "a": 12, "next_mix": 10},
}
for _r in "tsmy":
    INCS[f"{_r}_free"] = dict(INCS[f"{_r}_full"])
INCS["ta_free"] = {"qkv0": 2, "a": NA * HJ, "b": NB * HJ, "next_mix": 3}
INCS["t_free"] |= {"qkv0": 2, "a": 0, "b": 0, "next_mix": 3 + 2 * NT}
START = 2


def kind_of(it):
    return "first" if it is None else "body" if not isinstance(it, int) else "second" if it == 0 else "last"


def incs(sem, stage, kind):
    table = INCS[sem]
    if stage in ("turn", "mix"):
        return sum(table.get(p, 0) for p in parts(stage, kind))
    there = kind != "first" if stage in OWN else kind != "last"
    return table.get(stage, 0) if there else 0


def before(sem, stage, kind):
    return sum(incs(sem, s, kind) for s in STAGES[:STAGES.index(stage)])


def total(sem, kind):
    return before(sem, "mix", kind) + incs(sem, "mix", kind)


PER = {s: total(s, "body") for s in INCS}


def upto(sem, it, stage, n):
    here = START + before(sem, stage, kind_of(it)) + n
    if it is None:
        return here
    here += total(sem, "first")
    return here if kind_of(it) == "second" else it * PER[sem] + (total(sem, "second") - PER[sem] + here)


def att_t(layer, n):
    return ("attn1b", n - 2 * NT) if layer and n >= 2 * NT else (f"attn{layer}", n)


def att_m(layer, p):
    return ("attn1b", p - 2) if layer and p >= 2 else (f"attn{layer}", p)


def first_expert(stage):
    return NA if stage == "turn" else 0


def t_slot(stage, n):
    return n % 2


def s_bank(stage, n):
    return n % 2


def q_from(layer, kt):
    return kt * P if layer else 0


def build(nc, x_tok, x_t, consts, hots, masks, w_qkv0, b_qkv0, w_p0, b_p0, rel_h, rel_w, w_qkv1, w_p1, gate_w, gate_b,
          w1, b1, w2, b2, out):
    with ExitStack() as ctx:
        def sb(name, shape, dt=F32):
            return ctx.enter_context(nc.sbuf_tensor(name, shape, dt))

        def ps(name, shape):
            return ctx.enter_context(nc.psum_tensor(name, shape, F32))

        sems = {n: ctx.enter_context(nc.semaphore(n)) for n in INCS}
        xt_in = sems["xt_in"]
        x0_in = sems["x0_in"]
        out_done = sems["out_done"]
        gstat = sems["gstat"]
        xnt_gn = sems["xnt_gn"]
        var_ready = sems["var_ready"]
        ln_var = sems["ln_var"]
        rs0 = sems["rs0"]
        t_full = sems["t_full"]
        s_full = sems["s_full"]
        m_full = sems["m_full"]
        y_full = sems["y_full"]
        o_free = sems["o_free"]
        lvl1 = sems["lvl1"]
        lvl2 = sems["lvl2"]
        lvl3 = sems["lvl3"]
        pool_chain = sems["pool_chain"]
        lvl3_k1 = sems["lvl3_k1"]
        wide3 = sems["wide3"]
        spill_q = sems["spill_q"]
        spill_k = sems["spill_k"]
        qr_in = sems["qr_in"]
        ab_in = sems["ab_in"]
        l1_in = sems["l1_in"]
        l1_first = sems["l1_first"]
        rel_lead = sems["rel_lead"]
        rowmax = sems["rowmax"]
        gsum_full, gsum_free = sems["gsum_full"], sems["gsum_free"]
        negmax_in = sems["negmax_in"]
        p_used = sems["p_used"]
        ta_free = sems["ta_free"]
        h_used = sems["h_used"]
        au_in = sems["au_in"]
        lnl = sems["lnl"]
        il0 = sems["il0"]
        att_ready = sems["att_ready"]
        xn_tok_ready = sems["xn_tok_ready"]
        gate_max_ready = sems["gate_max_ready"]
        gate_exp_ready = sems["gate_exp_ready"]
        dve_chain = sems["dve_chain"]
        t_free = sems["t_free"]
        s_free = sems["s_free"]
        m_free = sems["m_free"]
        y_free = sems["y_free"]
        const_in = ctx.enter_context(nc.semaphore("const_in"))
        setup = ctx.enter_context(nc.semaphore("setup"))
        first_x = ctx.enter_context(nc.semaphore("first_x"))

        cst = sb("cst", [P, C_END])
        ident = cst[:, C_ID:C_ID + P]
        group = cst[0:C, C_GRP:C_GRP + C]
        ident_b = sb("ident_b", [P, P], BF16)
        mask_q = sb("mask_q", [P, P], BF16)
        mask_k = sb("mask_k", [P, P], BF16)
        wqkv = [sb("wqkv0", [C + 1, 3 * C]), sb("wqkv1", [C, 3 * C])]
        wp = [sb("wp0", [C + 1, C]), sb("wp1", [C, C])]
        gw = sb("gw", [C + 1, NE])
        w1s = sb("w1s", [C + 1, NE * HID])
        w2s = sb("w2s", [P, NE * HJ, C])
        b2s = sb("b2s", [C, NE])
        relf = sb("relf", [C, 2, WIN])
        relr = sb("relr", [C, 2, WIN])
        rell = sb("rell", [C, 2, WIN], BF16)
        relt = sb("relt", [C, 2, WIN], BF16)

        x0 = sb("x0", [P, NT, C])
        x1 = sb("x1", [P, NT, C])
        x2 = sb("x2", [P, NT, C])
        xn_tok = sb("xn_tok", [P, NT, C])
        xnt = sb("xnt", [C + 1, T])
        xg = sb("xg", [C + 1, T])
        xf = sb("xf", [C + 1, T])
        split = sb("split", [C, 2, 3, T], BF16)
        resid = sb("resid", [C, T])
        qr = sb("qr", [C + 1, NH, T], BF16)
        kr = sb("kr", [C + 1, NH, T], BF16)
        qa = sb("qa", [P, NH, T], BF16)
        ka = sb("ka", [P, NH, T], BF16)
        qb = sb("qb", [C + 1, NH, T], F32R)
        kb = sb("kb", [C + 1, NH, T], F32R)
        qb_raw, kb_raw = qb[:, :, :].bitcast(F32), kb[:, :, :].bitcast(F32)
        vs = [sb(f"v{l}", [P, NT, NH, 2 * HD]) for l in (0, 1)]
        probs = sb("probs", [P, 4, T])
        wide = qb[0:C, 0:4, :]
        mx = [sb(f"mx{l}", [P, 2, 2 * NT, NC]) for l in (0, 1)]
        mrow = sb("mrow", [P, 2, 2 * NT])
        negm = [sb("negr", [2 * NT, 2, P], F32R), sb("negb", [2 * NT, 2, P], BF16)]
        negm_raw = [negm[0][:, :, :].bitcast(F32), negm[1]]
        ot = sb("ot", [P, PAIRS, HALF])
        au = sb("au", [C, T])
        lb = sb("lb", [C, T])
        il = sb("il", [C, T])
        att = sb("att", [C + 1, T])
        hbuf = probs
        yts = {"mix": qa[0:C, 0:2, :].rearrange("c h t -> c (h t)").bitcast(F32),
               "turn": kr[0:C, 0:2, :].rearrange("c h t -> c (h t)").bitcast(F32)}
        res_of = (resid, il)
        gs6 = sb("gs6", [C, 2, 6])
        gsm = sb("gsm", [C, 16])
        gst = sb("gst", [C, 2])
        gm = sb("gm", [C, 8])
        st6 = sb("st6", [P, NT, 6])
        sm = sb("sm", [P, 12, NT])
        g4 = sb("g4", [P, 5, NT, NE])
        g16 = sb("g16", [P, 2, NT, NE, NE])
        gden = sb("gden", [P, 4, NT])

        psT = ps("psT", [P, 2, T])
        psS = ps("psS", [P, 2, HALF])
        psOM = ps("psOM", [P, 2, HALF])
        psO, psM = psOM[:, 0, :], psOM[:, 1, :]

        scr = nc.dram_tensor("scr", [C, 2, 3, T], BF16).ap()
        scr32 = nc.dram_tensor("scr32", [C, 4, T], F32).ap()
        scr_d = scr.rearrange("(h d) s l t -> d s l h t", d=HD)
        scr1 = nc.dram_tensor("scr1", [C, 2, 3, T], BF16).ap()
        scr1_d = scr1.rearrange("(h d) s l t -> d s l h t", d=HD)
        scr32_d = scr32.rearrange("(h d) s t -> d s h t", d=HD)

        loads = [
            (cst[:, :], consts), (resid[0:2 * HS, :], hots), (probs[:, 0, 0:2 * P], masks),
            (wqkv[0][0:C, :], w_qkv0), (wqkv[0][C:C + 1, :], b_qkv0), (wqkv[1][:, :], w_qkv1),
            (wp[0][0:C, :], w_p0), (wp[0][C:C + 1, :], b_p0), (wp[1][:, :], w_p1), (gw[0:C, :], gate_w),
            (gw[C:C + 1, :], gate_b),
            (w1s[0:C, :].rearrange("c (e h) -> c e h", e=NE), w1.rearrange("e c h -> c e h")),
            (w1s[C:C + 1, :], b1), (w2s[:, :, :], w2.rearrange("e (j p) c -> p (e j) c", p=P)), (b2s[:, :], b2),
            (relf[:, 0, :], rel_h), (relf[:, 1, :], rel_w),
        ]
        n_setup = 32

        block = ctx.enter_context(nc.Block())

        @block.sync
        def _(sp):
            for sem in sems.values():
                sp.sem_inc(sem, START)
            for dst, src in loads:
                sp.dma_start(dst, src).then_inc(const_in, 16)

            def fill_slots(dst, src_d, s, slots, heads, done):
                for n, l in enumerate(slots):
                    sp.dma_start(dst[n * HD:(n + 1) * HD, heads, :], src_d[:, s, l, heads]).then_inc(done, 16)

            def put_max(it, layer, p):
                st, n = att_m(layer, p)
                sp.wait_ge(m_free, upto("m_free", it, st, n + 1))
                row = (qb_raw, qr)[layer][C:C + 1, 2 * p:2 * p + 2, :]
                sp.dma_start(row.rearrange("o h (t q) -> o (h t) q", q=P),
                             negm_raw[layer][:, p % 2, :]).then_inc(negmax_in, 16)

            def gather(it, layer, p):
                sp.wait_ge(o_free, upto("o_free", it, f"attn{layer}", p + 1))
                for hh in range(2):
                    for c in range(NC):
                        h, j = 2 * p + hh, 32 * (2 * hh + c)
                        rows, cols = slice(h * HD, (h + 1) * HD), slice(c * HALF, (c + 1) * HALF)
                        sp.dma_start(au[rows, cols], ot[j:j + HD, p, :]).then_inc(au_in, 16)
                        sp.dma_start(lb[rows, cols], ot[j + HD:j + 2 * HD, p, :]).then_inc(au_in, 16)

            def spill0(it):
                for s, spill in ((0, spill_q), (1, spill_k)):
                    sp.wait_ge(lvl3, upto("lvl3", it, "qkv0", s + 1))
                    sp.dma_start(scr[:, s], split[:, s]).then_inc(spill, 16)
                    sp.wait_ge(wide3, upto("wide3", it, "qkv0", s + 1))
                    sp.dma_start(scr32[:, 2 * s:2 * s + 2], qb_raw[0:C, 2 * s:2 * s + 2, :]).then_inc(spill, 16)

            def q_operands(it):
                sp.wait_ge(spill_q, upto("spill_q", it, "qkv0", 32))
                fill_slots(qa, scr_d, 0, Q_SLOTS[:4], slice(0, NH), ab_in)
                sp.wait_ge(spill_k, upto("spill_k", it, "qkv0", 32))
                for n in range(2):
                    sp.dma_start(qb_raw[64 + n * HD:64 + (n + 1) * HD, :, :], scr32_d[:, n]).then_inc(ab_in, 16)

            def k_operands(it):
                fill_slots(ka, scr_d, 1, K_SLOTS[:4], slice(0, NH), ab_in)
                for n in range(2):
                    sp.dma_start(kb_raw[64 + n * HD:64 + (n + 1) * HD, :, :], scr32_d[:, 3 - n]).then_inc(ab_in, 16)

            def bias_operand(it, heads):
                fill_slots(qr, scr_d, 0, Q_SLOTS, heads, qr_in)

            def slots1(it):
                sp.wait_ge(lvl3, upto("lvl3", it, "mix", 1))
                sp.dma_start(scr1[:, 0], split[:, 0]).then_inc(spill_q, 16)
                sp.wait_ge(lvl3_k1, upto("lvl3_k1", it, "mix", 1))
                sp.dma_start(scr1[:, 1], split[:, 1]).then_inc(spill_k, 16)
                sp.wait_ge(spill_q, upto("spill_q", it, "mix", 16))
                fill_slots(qr, scr1_d, 0, Q_SLOTS, slice(0, 2), l1_first)
                sp.wait_ge(spill_k, upto("spill_k", it, "mix", 16))
                fill_slots(kr, scr1_d, 1, K_SLOTS, slice(0, 2), l1_first)
                fill_slots(qr, scr1_d, 0, Q_SLOTS, slice(2, NH), l1_in)
                fill_slots(kr, scr1_d, 1, K_SLOTS, slice(2, NH), l1_in)

            def attention1(it):
                body = kind_of(it) != "last"
                put_max(it, 1, 0)
                put_max(it, 1, 1)
                gather(it, 1, 0)
                if body:
                    spill0(it)
                put_max(it, 1, 2)
                gather(it, 1, 1)
                if body:
                    bias_operand(it, slice(0, 4))
                    q_operands(it)
                if body:
                    sp.wait_ge(o_free, upto("o_free", it, "attn1", PAIRS))
                    bias_operand(it, slice(4, NH))
                    k_operands(it)
                gather(it, 1, 2)

            def attention0(it, row):
                sp.wait_ge(t_free, upto("t_free", it, "attn0", 0))
                sp.dma_start(x0[:, :, :], x_tok[row]).then_inc(x0_in, 16)
                for p in range(PAIRS + 1):
                    if p < PAIRS:
                        put_max(it, 0, p)
                    if p >= 1:
                        gather(it, 0, p - 1)
                slots1(it)
                sp.dma_start(xg[0:C, :], x_t[row + 1]).then_inc(xt_in, 16)

            def store(it, stage, row):
                n = NE if stage == "mix" else NB
                sp.wait_ge(y_free, upto("y_free", it, stage, n))
                sp.dma_start(out[row], x2[:, :, :]).then_inc(out_done, 16)

            sp.wait_ge(setup, n_setup)
            sp.dma_start(xg[0:C, :], x_t[0]).then_inc(first_x, 16)
            spill0(None)
            q_operands(None)
            bias_operand(None, slice(0, 4))
            bias_operand(None, slice(4, NH))
            k_operands(None)
            attention0(None, 0)
            attention1(0)
            attention0(0, 1)
            with sp.Fori(1, B - 1) as it:
                attention1(it)
                store(it, "turn", it - 1)
                attention0(it, it + 1)
            attention1(B - 1)
            store(B - 1, "turn", B - 2)
            store(B - 1, "mix", B - 1)
            sp.wait_ge(out_done, START + 16 * B)
            sp.wait_ge(xt_in, START + 16 * B)

        @block.tensor
        def _(pe):
            mm = nc.tensor.matmul

            def take_t(it, stage, n):
                pe.wait_ge(t_free, upto("t_free", it, stage, n - 1))
                return psT[:, t_slot(stage, n), :]

            def take_mixed(it, stage, what):
                all_fills = fills(stage, kind_of(it))
                n = all_fills.index(what)
                until = all_fills[:n - 1] if n >= 2 else []
                act = len([x for x in until if by_act(x)])
                if until and by_act(until[-1]):
                    pe.wait_ge(ta_free, upto("ta_free", it, stage, act))
                else:
                    pe.wait_ge(t_free, upto("t_free", it, stage, len(until) - act))
                return psT[:, t_slot(stage, n), :]

            def qk(layer, o, s):
                k, w, x = C + 1 - layer, wqkv[layer], (xg, xnt)[layer]
                for c in range(NC):
                    last = mm(o[0:C, c * HALF:(c + 1) * HALF], w[0:k, s * C:(s + 1) * C],
                              x[0:k, c * HALF:(c + 1) * HALF], start=True, stop=True)
                last.then_inc(t_full, 1)

            def val(layer, o, half):
                k, w, x = C + 1 - layer, wqkv[layer], (xg, xnt)[layer]
                for i in range(4):
                    t = 4 * half + i
                    last = mm(o[:, i * C:(i + 1) * C], x[0:k, t * P:(t + 1) * P], w[0:k, 2 * C:3 * C],
                              start=True, stop=True)
                last.then_inc(t_full, 1)

            def bias(it, g):
                o = take_mixed(it, "turn", ("rel", g))
                q_cols = qr[0:C, :, :].rearrange("c h (a b) -> c h a b", b=WS)
                for i in range(REL_STEP):
                    r = REL_STEP * g + i
                    window = slice(HS - 1 - r, 2 * HS - 1 - r)
                    mm(o[0:HS, 256 * i:256 * i + NH * WS], relt[:, 0, window], qr[0:C, :, r * WS:(r + 1) * WS],
                       start=True, stop=True)
                    last = mm(o[HS:2 * HS, 256 * i:256 * i + NH * HS], relt[:, 1, window], q_cols[:, :, :, r],
                              start=True, stop=True)
                last.then_inc(t_full, 1)

            def attention(it, layer):
                st, v = f"attn{layer}", vs[layer]

                def max_scores(fill):
                    h, t, kc = MAX_STEPS[layer][fill]
                    n = max_cols(layer, t, kc)
                    pe.wait_ge(s_free, upto("s_free", it, st, fill - 1))
                    bank = psS[:, s_bank(st, fill), :]
                    q, k, rows = ((qa, ka, P), (qr, kr, C))[layer]
                    diagonal = layer == 1 and (t + 1) * P <= (kc + 1) * HALF
                    last = mm(bank[:, 0:n], q[0:rows, h, t * P:(t + 1) * P], k[0:rows, h, kc * HALF:kc * HALF + n],
                              start=True, stop=not diagonal)
                    if diagonal:
                        last = mm(bank[:, n - P:n], ident_b[:, :], mask_q[:, :], start=False, stop=True)
                    last.then_inc(s_full, 1)

                def transpose_max(p):
                    if p == 0:
                        pe.wait_ge(t_free, upto("t_free", it, st, 0))
                    else:
                        pe.wait_ge(rowmax, upto("rowmax", it, st, p))
                    ms, n = att_m(layer, p)
                    pe.wait_ge(m_free, upto("m_free", it, ms, n))
                    mm(psM[0:2 * NT, 0:P], mrow[:, p % 2, :], ident, is_transpose=True, start=True,
                       stop=True).then_inc(m_full, 1)

                def scores(p, kt, hh):
                    h, q0, ks = 2 * p + hh, q_from(layer, kt), slice(kt * P, (kt + 1) * P)
                    o = take_t(it, *att_t(layer, (p * NT + kt) * 2 + hh))
                    for c in range(NC):
                        a, b = max(q0, c * HALF), (c + 1) * HALF
                        if a >= b:
                            continue
                        if layer == 0:
                            mm(o[:, a:b], ka[:, h, ks], qa[:, h, a:b], start=True, stop=False)
                            last = mm(o[:, a:b], kb[:, h, ks], qb[:, h, a:b], start=False, stop=True)
                        else:
                            last = mm(o[:, a:b], kr[:, h, ks], qr[:, h, a:b], start=True, stop=a != q0)
                            if a == q0:
                                last = mm(o[:, a:a + P], ident_b[:, :], mask_k[:, :], start=False, stop=True)
                    last.then_inc(t_full, 1)

                def values(p, kt):
                    q0 = q_from(layer, kt)
                    if kt == 0:
                        pe.wait_ge(o_free, upto("o_free", it, st, p))
                    for hh in range(2):
                        ts, n = att_t(layer, (p * NT + kt) * 2 + hh)
                        pe.wait_ge(t_free, upto("t_free", it, ts, n + 1))
                        for c in range(NC):
                            a, j = max(q0, c * HALF), 32 * (2 * hh + c)
                            if a >= (c + 1) * HALF:
                                continue
                            end = NT if layer == 0 else (c + 1) * HALF // P
                            last = mm(psO[j:j + 2 * HD, a - c * HALF:HALF], v[:, kt, 2 * p + hh, :],
                                      probs[:, (2 * kt + hh) % 4, a:(c + 1) * HALF], start=kt == 0, stop=kt == end - 1)
                        last.then_inc(p_used, 1)

                n = PER_PAIR[layer]
                pe.wait_ge(y_free, upto("y_free", it, st, 0))
                transpose_max(0)
                if layer == 1:
                    pe.wait_ge(l1_in, upto("l1_in", it, "attn1", 0))
                for fill in range(LEAD):
                    max_scores(fill)
                if layer == 1 and kind_of(it) in ("second", "body"):
                    group_means(it)
                    pe.wait_ge(gsum_free, upto("gsum_free", it, "gn", 1))
                for p in range(PAIRS):
                    next_q = layer == 1 and p == 1 and kind_of(it) in ("second", "body")
                    ahead = range(p * n + (LEAD if p == 0 or next_q else 0), (p + 1) * n) if p + 1 < PAIRS else ()
                    cut = [min(len(ahead), len(ahead) * i // (2 * NT - 4)) for i in range(2 * NT + 1)]
                    if next_q:
                        next_qkv(it, max_scores, n)
                    pe.wait_ge(negmax_in, upto("negmax_in", it, st, 16 * (p + 1)))
                    for kt in range(NT):
                        for hh in range(2):
                            scores(p, kt, hh)
                            if hh == 1 and kt >= 1:
                                values(p, kt - 1)
                            for fill in ahead[cut[2 * kt + hh]:cut[2 * kt + hh + 1]]:
                                max_scores(fill)
                        if kt == NT - 2 and p + 1 < PAIRS:
                            transpose_max(p + 1)
                        if layer == 0 and p == PAIRS - 1 and it is not None:
                            if kt == 1:
                                res_norm(it)
                            elif kt == NT - 2:
                                tr_norm(it)
                    values(p, NT - 1)

            def res_norm(it):
                pe.wait_ge(att_ready, upto("att_ready", it, "turn", 1))
                for b in range(NC):
                    pe.wait_ge(s_free, upto("s_free", it, "norm", b - 1))
                    for i in range(4):
                        t = 4 * b + i
                        last = mm(psS[:, b, i * C:(i + 1) * C], att[0:C, t * P:(t + 1) * P], wp[1][:, :], start=True,
                                  stop=True)
                    last.then_inc(s_full, 1)

            def tr_norm(it):
                pe.wait_ge(xn_tok_ready, upto("xn_tok_ready", it, "norm", 1))
                for b in range(NC):
                    pe.wait_ge(s_free, upto("s_free", it, "norm", b + 1))
                    for i in range(4):
                        last = mm(psS[0:C, b, i * P:(i + 1) * P], xn_tok[:, 4 * b + i, :], ident, is_transpose=True,
                                  start=True, stop=True)
                    last.then_inc(s_full, 1)

            def res(it, stage, layer):
                k = C + 1 - layer
                pe.wait_ge(att_ready, upto("att_ready", it, stage, 1))
                o = take_mixed(it, stage, ("res", layer))
                for t in range(NT):
                    a = (t // 4) * HALF + (t % 4) * C
                    last = mm(o[:, a:a + C], att[0:k, t * P:(t + 1) * P], wp[layer][0:k, :], start=True, stop=True)
                last.then_inc(t_full, 1)

            def tr(it, stage, layer):
                pe.wait_ge(xn_tok_ready, upto("xn_tok_ready", it, stage, 1))
                o = take_mixed(it, stage, ("tr", layer))
                for t in range(NT):
                    last = mm(o[0:C, t * P:(t + 1) * P], xn_tok[:, t, :], ident, is_transpose=True, start=True,
                              stop=True)
                last.then_inc(t_full, 1)

            def gate_scores(it):
                pe.wait_ge(s_free, upto("s_free", it, "mix", 0))
                pe.wait_ge(m_free, upto("m_free", it, "mix", 0))
                for t in range(NT):
                    last = mm(psM[:, t * NE:(t + 1) * NE], xf[:, t * P:(t + 1) * P], gw[:, :], start=True, stop=True)
                last.then_inc(m_full, 1)

            def up(it, stage, n):
                o, (x, j) = take_mixed(it, stage, ("up", n)), divmod(n, HJ)
                a = x * HID + j * P
                for c in range(NC):
                    last = mm(o[:, c * HALF:(c + 1) * HALF], w1s[:, a:a + P], xf[:, c * HALF:(c + 1) * HALF],
                              start=True, stop=True)
                last.then_inc(t_full, 1)

            def down(it, stage, n):
                x, j = divmod(n, HJ)
                if j == 0:
                    pe.wait_ge(s_free, upto("s_free", it, stage, 2 * (x - first_expert(stage))))
                fs = fills(stage, kind_of(it))
                written = len([f for f in fs[:fs.index(("up", n)) + 1] if by_act(f)])
                pe.wait_ge(ta_free, upto("ta_free", it, stage, written))
                for c in range(NC):
                    last = mm(psS[0:C, c, :], w2s[:, n, :], hbuf[:, n % 4, c * HALF:(c + 1) * HALF], start=j == 0,
                              stop=j == HJ - 1)
                    if j == HJ - 1:
                        last.then_inc(s_full, 1)
                    elif c == NC - 1:
                        last.then_inc(h_used, 1)

            def back(it, stage, x):
                i = x - first_expert(stage)
                pe.wait_ge(s_free, upto("s_free", it, stage, 2 * i + 2))
                pe.wait_ge(y_free, upto("y_free", it, stage, i))
                if i == 0:
                    pe.wait_ge(m_free, upto("m_free", it, stage, 1 if stage == "mix" else 0))
                    pe.wait_ge(o_free, upto("o_free", it, stage, 0))
                for t in range(NT):
                    last = mm(psOM[:, t // 4, (t % 4) * C:(t % 4 + 1) * C], yts[stage][:, t * P:(t + 1) * P],
                              ident[0:C, 0:C], is_transpose=True, start=True, stop=True)
                last.then_inc(y_full, 1)

            def first_maxima(it, stage, i):
                o, (h, t) = take_mixed(it, stage, ("max", i)), divmod(i, NT)
                q, k, rows, layer = (qa, ka, P, 0) if stage == "turn" else (qr, kr, C, 1)
                for c in range(NC):
                    n = max_cols(layer, t, c)
                    if not n:
                        continue
                    diagonal = layer == 1 and n < HALF or (t + 1) * P == (c + 1) * HALF and layer == 1
                    last = mm(o[:, c * HALF:c * HALF + n], q[0:rows, h, t * P:(t + 1) * P],
                              k[0:rows, h, c * HALF:c * HALF + n], start=True, stop=not diagonal)
                    if diagonal:
                        last = mm(o[:, c * HALF + n - P:c * HALF + n], ident_b[:, :], mask_q[:, :], start=False,
                                  stop=True)
                last.then_inc(t_full, 1)

            def turn(it):
                for what, n in steps("turn", kind_of(it)):
                    if what == "up":
                        up(it, "turn", n)
                    elif what == "down":
                        down(it, "turn", n)
                    elif what == "back":
                        back(it, "turn", n)
                    elif what == "rel":
                        if n == 0:
                            pe.wait_ge(qr_in, upto("qr_in", it, "turn", 0))
                        bias(it, n)
                    elif what == "max":
                        if n == 0:
                            pe.wait_ge(ab_in, upto("ab_in", it, "turn", 0))
                            pe.wait_ge(t_free, upto("t_free", it, "turn", REL_FILLS))
                        first_maxima(it, "turn", n)

            def mix(it):
                if it is not None:
                    gate_scores(it)
                for what, n in steps("mix", kind_of(it)):
                    if what == "up":
                        up(it, "mix", n)
                    elif what == "down":
                        down(it, "mix", n)
                    elif what == "back":
                        back(it, "mix", n)
                    elif what == "res":
                        res(it, "mix", n)
                    elif what == "tr":
                        tr(it, "mix", n)
                    elif what == "qk":
                        if n == 0:
                            fs = fills("mix", kind_of(it))
                            written = len([f for f in fs[:fs.index(("tr", 0)) + 1] if by_act(f)])
                            pe.wait_ge(ta_free, upto("ta_free", it, "mix", written))
                        qk(1, take_mixed(it, "mix", ("qk", n)), n)
                    elif what == "val":
                        val(1, take_mixed(it, "mix", ("val", n)), n)
                    elif what == "max":
                        if n == 0:
                            pe.wait_ge(l1_first, upto("l1_first", it, "mix", 192))
                        first_maxima(it, "mix", n)

            def group_means(it):
                pe.wait_ge(gstat, upto("gstat", it, "gn", 1))
                mm(psO[0:C, 0:2], group, gst[:, :], start=True, stop=True).then_inc(gsum_full, 1)

            def next_qkv(it, max_scores=None, first=0):
                def maxima(a, b):
                    for fill in range(first + a, first + b) if max_scores else ():
                        max_scores(fill)

                pe.wait_ge(xnt_gn, upto("xnt_gn", it, "gn", 1))
                qk(0, take_t(it, "qkv0", 0), 0)
                maxima(0, 2)
                qk(0, take_t(it, "qkv0", 1), 1)
                val(0, take_t(it, "qkv0", 2), 0)
                maxima(2, 5)
                val(0, take_t(it, "qkv0", 3), 1)
                maxima(5, LEAD)
                pe.wait_ge(ta_free, upto("ta_free", it, "qkv0", 2))

            pe.wait_ge(const_in, 16 * len(loads))
            pe.wait_ge(setup, n_setup)
            group_means(None)
            next_qkv(None)
            turn(None)
            attention(None, 0)
            mix(None)
            attention(0, 1)
            turn(0)
            attention(0, 0)
            mix(0)
            with pe.Fori(1, B - 1) as it:
                attention(it, 1)
                turn(it)
                attention(it, 0)
                mix(it)
            attention(B - 1, 1)
            turn(B - 1)
            res_norm(B - 1)
            tr_norm(B - 1)
            mix(B - 1)

        def rel_views(dst, base, g, o):
            o = o.rearrange("p (i r) -> p i r", r=256)[:, :, 0:NH * HS]
            r = slice(REL_STEP * g, REL_STEP * (g + 1))
            return ((dst[base:base + HS].rearrange("p h (a b) -> p a h b", b=WS)[:, r],
                     o[0:HS].rearrange("p i (h b) -> p i h b", h=NH)),
                    (dst[base + HS:base + 2 * HS].rearrange("p h (a b) -> p h a b", b=WS)[:, :, :, r],
                     o[HS:2 * HS].rearrange("p i (h a) -> p h a i", h=NH)))

        @block.scalar
        def _(act):
            A = nc.scalar.activation

            def rstd_guess(it, stage, v, lnv, y):
                act.wait_ge(var_ready, upto("var_ready", it, stage, 1))
                A(lnv, v, ACT.Ln).then_inc(ln_var, 1)
                act.wait_ge(ln_var, upto("ln_var", it, stage, 1))
                A(y, lnv, ACT.Exp, scale=-0.5).then_inc(rs0, 1)

            def levels_a(it, stage, layer, s):
                n = s if layer == 0 else fills(stage, kind_of(it)).index(("qk", s))
                if s == 0:
                    act.wait_ge(spill_q, upto("spill_q", it, stage, 0))
                    act.wait_ge(spill_k, upto("spill_k", it, stage, 0))
                act.wait_ge(t_full, upto("t_full", it, stage, n + 1))
                A(split[:, s, 0, :], psT[0:C, t_slot(stage, n), :], ACT.Copy, scale=(1.0, SCALE)[s]).then_inc(lvl1, 1)

            def keep_values(it, stage, layer, b):
                n = 2 + b if layer == 0 else fills(stage, kind_of(it)).index(("val", b))
                act.wait_ge(t_full, upto("t_full", it, stage, n + 1))
                A(vs[layer][:, 4 * b:4 * b + 4, :, 0:HD],
                  psT[:, t_slot(stage, n), 0:4 * C].rearrange("p (t h d) -> p t h d", t=4, h=NH),
                  ACT.Copy).then_inc(ta_free, 1)

            def levels_b(it, stage, layer, s):
                freed = s + 1
                if layer == 1:
                    fs = fills(stage, kind_of(it))
                    freed = len([f for f in fs[:fs.index(("qk", s)) + 1] if not by_act(f)])
                act.wait_ge(t_free, upto("t_free", it, stage, freed))
                A(split[:, s, 1, :], res_of[s][0:C, :], ACT.Copy).then_inc(lvl2, 1)
                if layer == 0:
                    act.wait_ge(lvl1, upto("lvl1", it, stage, s + 1))
                    A(wide[:, 2 * s, :], split[:, s, 0, :], ACT.Copy)

            def levels_c(it, s):
                act.wait_ge(lvl3, upto("lvl3", it, "qkv0", s + 1))
                A(wide[:, 2 * s + 1, :], split[:, s, 2, :], ACT.Copy).then_inc(wide3, 1)

            def attention(it, layer):
                st = f"attn{layer}"

                def neg_max(p):
                    ms, n = att_m(layer, p)
                    act.wait_ge(m_full, upto("m_full", it, ms, n + 1))
                    act.wait_ge(negmax_in, upto("negmax_in", it, st, 16 * max(p - 1, 0)))
                    A(negm[layer][:, p % 2, :], psM[0:2 * NT, 0:P], ACT.Copy, scale=-1.0).then_inc(m_free, 1)

                def evacuate(p):
                    if layer == 0 and p == 0 and it is not None:
                        act.wait_ge(att_ready, upto("att_ready", it, "attn0", 0))
                    act.wait_ge(p_used, upto("p_used", it, st, 2 * NT * (p + 1)))
                    act.wait_ge(au_in, upto("au_in", it, st, 0))
                    A(ot[:, p, :], psO, ACT.Copy).then_inc(o_free, 1)

                next_q = layer == 1 and kind_of(it) in ("second", "body")
                neg_max(0)
                if next_q:
                    rstd_guess(it, "gn", gm[:, 3:4], gm[:, 4:5], gm[:, 5:6])
                for p in range(PAIRS):
                    if next_q and p == 1:
                        for s in range(2):
                            levels_a(it, "qkv0", 0, s)
                        for b in range(2):
                            keep_values(it, "qkv0", 0, b)
                    for kt in range(NT):
                        for hh in range(2):
                            n = (p * NT + kt) * 2 + hh
                            ts, m = att_t(layer, n)
                            act.wait_ge(t_full, upto("t_full", it, ts, m + 1))
                            act.wait_ge(p_used, upto("p_used", it, st, max(n - 3, 0)))
                            q0 = q_from(layer, kt)
                            A(probs[:, n % 4, q0:T], psT[:, t_slot(ts, m), q0:T], ACT.Exp).then_inc(t_free, 1)
                        if kt == 0 and p >= 1:
                            evacuate(p - 1)
                        if kt == NT - 2 and p + 1 < PAIRS:
                            neg_max(p + 1)
                        if layer == 0 and p == PAIRS - 1 and it is not None and kt == 2:
                            rstd_guess(it, "norm", sm[:, 5, :], sm[:, 6, :], sm[:, 7, :])
                        if next_q and p == 1 and kt in (0, 1):
                            levels_b(it, "qkv0", 0, kt)
                        if next_q and p == 1 and kt in (2, 3):
                            levels_c(it, kt - 2)
                evacuate(PAIRS - 1)

            def den(it, stage):
                act.wait_ge(au_in, upto("au_in", it, stage, 0))
                A(il[:, :], lb[:, :], ACT.Ln).then_inc(lnl, 1)
                act.wait_ge(lnl, upto("lnl", it, stage, 1))
                A(il[:, :], il[:, :], ACT.Exp, scale=-1.0).then_inc(il0, 1)

            def tr(it, stage, layer):
                n = fills(stage, kind_of(it)).index(("tr", layer))
                act.wait_ge(t_full, upto("t_full", it, stage, n + 1))
                A(xnt[0:C, :], psT[0:C, t_slot(stage, n), :], ACT.Copy).then_inc(ta_free, 1)

            def gelu(it, stage, n):
                fill = fills(stage, kind_of(it)).index(("up", n))
                used = n - 4
                done = used // HJ - first_expert(stage)
                if done >= 0 and used % HJ == HJ - 1:
                    act.wait_ge(s_full, upto("s_full", it, stage, 2 * (done + 1)))
                elif done >= 0:
                    act.wait_ge(h_used, upto("h_used", it, stage, (HJ - 1) * done + used % HJ + 1))
                act.wait_ge(t_full, upto("t_full", it, stage, fill + 1))
                A(hbuf[:, n % 4, :], psT[:, t_slot(stage, fill), :], ACT.Gelu).then_inc(ta_free, 1)

            def expert_out(it, stage, x):
                i = x - first_expert(stage)
                act.wait_ge(y_full, upto("y_full", it, stage, i))
                for c in range(NC):
                    act.wait_ge(s_full, upto("s_full", it, stage, 2 * i + c + 1))
                    A(yts[stage][:, c * HALF:(c + 1) * HALF], psS[0:C, c, :], ACT.Identity,
                      bias=b2s[:, x:x + 1]).then_inc(s_free, 1)

            def turn(it):
                for what, n in steps("turn", kind_of(it)):
                    if what == "down" and n % HJ == HJ - 1:
                        expert_out(it, "turn", n // HJ)
                    elif what == "ln":
                        den(it, "turn")
                    elif what == "up":
                        gelu(it, "turn", n)
                    elif what == "rel":
                        fill = fills("turn", kind_of(it)).index((what, n))
                        if n == 0:
                            act.wait_ge(spill_k, upto("spill_k", it, "turn", 0))
                        act.wait_ge(t_full, upto("t_full", it, "turn", fill + 1))
                        rows, cols = rel_views(qa, 64, n, psT[:, t_slot("turn", fill), :])
                        A(rows[0], rows[1], ACT.Copy).then_inc(rel_lead, 1)
                        A(cols[0], cols[1], ACT.Copy).then_inc(rel_lead, 1)

            def mix(it):
                if it is not None:
                    act.wait_ge(gate_max_ready, upto("gate_max_ready", it, "mix", 1))
                    A(g4[:, 1], g4[:, 0], ACT.Exp).then_inc(gate_exp_ready, 1)
                for what, n in steps("mix", kind_of(it)):
                    if what == "up":
                        gelu(it, "mix", n)
                    elif what == "down" and n % HJ == HJ - 1:
                        expert_out(it, "mix", n // HJ)
                    elif what == "ln":
                        den(it, "mix")
                    elif what == "nrm":
                        rstd_guess(it, "mix", sm[:, 5, :], sm[:, 6, :], sm[:, 7, :])
                    elif what == "tr":
                        tr(it, "mix", n)
                    elif what == "qk":
                        levels_a(it, "mix", 1, n)
                    elif what == "val":
                        keep_values(it, "mix", 1, n)
                    elif what == "lev":
                        for s in range(2):
                            levels_b(it, "mix", 1, s)

            act.wait_ge(const_in, 16 * len(loads))
            act.wait_ge(setup, n_setup)
            rstd_guess(None, "gn", gm[:, 3:4], gm[:, 4:5], gm[:, 5:6])
            for s in range(2):
                levels_a(None, "qkv0", 0, s)
            for b in range(2):
                keep_values(None, "qkv0", 0, b)
            for s in range(2):
                levels_b(None, "qkv0", 0, s)
            for s in range(2):
                levels_c(None, s)
            turn(None)
            attention(None, 0)
            mix(None)
            attention(0, 1)
            turn(0)
            attention(0, 0)
            mix(0)
            with act.Fori(1, B - 1) as it:
                attention(it, 1)
                turn(it)
                attention(it, 0)
                mix(it)
            attention(B - 1, 1)
            turn(B - 1)
            rstd_guess(B - 1, "norm", sm[:, 5, :], sm[:, 6, :], sm[:, 7, :])
            mix(B - 1)

        @block.gpsimd
        def _(pool):
            def level3(it, stage):
                for s in range(2 if stage == "qkv0" else 1):
                    pool.wait_ge(lvl2, upto("lvl2", it, stage, s + 1))
                    nc.gpsimd.tensor_tensor(split[:, s, 2, :], res_of[s][0:C, :], split[:, s, 1, :],
                                            ALU.subtract).then_inc(lvl3, 1)

            def den(it):
                g = nc.gpsimd
                pool.wait_ge(il0, upto("il0", it, "turn", 1))
                g.tensor_tensor(lb[:, :], lb[:, :], il[:, :], ALU.mult).then_inc(pool_chain, 1)
                pool.wait_ge(pool_chain, upto("pool_chain", it, "turn", 1))
                g.tensor_tensor(lb[:, :], lb[:, :], il[:, :], ALU.mult).then_inc(pool_chain, 1)
                g.tensor_tensor(att[0:C, :], il[:, :], il[:, :], ALU.add).then_inc(pool_chain, 1)
                pool.wait_ge(pool_chain, upto("pool_chain", it, "turn", 3))
                g.tensor_tensor(il[:, :], att[0:C, :], lb[:, :], ALU.subtract).then_inc(pool_chain, 1)
                pool.wait_ge(pool_chain, upto("pool_chain", it, "turn", 4))
                g.tensor_tensor(att[0:C, :], il[:, :], au[:, :], ALU.mult).then_inc(att_ready, 1)

            level3(None, "qkv0")
            level3(None, "mix")
            level3(0, "qkv0")
            den(0)
            level3(0, "mix")
            with pool.Fori(1, B - 1) as it:
                level3(it, "qkv0")
                den(it)
                level3(it, "mix")
            den(B - 1)

        @block.vector
        def _(dve):
            V = nc.vector
            done = [0]

            def ready(ins):
                done[0] += 1
                ins.then_inc(setup, 1)
                dve.wait_ge(setup, done[0])

            dve.wait_ge(const_in, 16 * len(loads))
            hot = resid[0:2 * HS, :]
            ready(V.tensor_copy(ident_b[:, :], ident))
            ready(V.tensor_copy(mask_q[:, :], probs[:, 0, 0:P]))
            ready(V.tensor_copy(mask_k[:, :], probs[:, 0, P:2 * P]))
            for h in range(NH):
                ready(V.tensor_copy(ka[64:128, h, :], hot))
                ready(V.tensor_copy(kb[0:64, h, :], hot))
            for ones in (kr[C:C + 1, :, :], kb[C:C + 1, :, :].bitcast(F32), xnt[C:C + 1, :],
                         xg[C:C + 1, :], xf[C:C + 1, :], att[C:C + 1, :],
                         vs[0][:, :, :, HD:2 * HD], vs[1][:, :, :, HD:2 * HD]):
                ready(V.memset(ones, 1.0))
            ready(V.memset(mx[0][:, :, :, :], -BIG))
            ready(V.memset(mx[1][:, :, :, :], -BIG))
            ready(V.tensor_copy(rell[:, :, :], relf[:, :, :]))
            ready(V.scalar_tensor_tensor(out=relr[:, :, :], in0=rell[:, :, :], scalar=cst[0:C, C_S1:C_S1 + 1],
                                         in1=relf[:, :, :], op0=ALU.mult, op1=ALU.add))
            ready(V.tensor_copy(rell[:, :, :], relr[:, :, :]))
            ready(V.scalar_tensor_tensor(out=relt[:, :, :], in0=rell[:, :, :], scalar=cst[0:C, C_S2:C_S2 + 1],
                                         in1=relr[:, :, :], op0=ALU.mult, op1=ALU.add))
            while done[0] < n_setup:
                ready(V.memset(gden[:, 3, :], 1.0))
            assert done[0] == n_setup, done[0]

            count = {}

            def link(it, stage, ins):
                key = (kind_of(it), stage)
                count[key] = count.get(key, 0) + 1
                ins.then_inc(dve_chain, 1)
                dve.wait_ge(dve_chain, upto("dve_chain", it, stage, count[key]))

            def newton(it, stage, v, y, tmp, out):
                dve.wait_ge(rs0, upto("rs0", it, stage, 1))
                link(it, stage, V.tensor_tensor(tmp, y, y, ALU.mult))
                link(it, stage, V.tensor_tensor(tmp, tmp, v, ALU.mult))
                link(it, stage, V.tensor_scalar(tmp, tmp, -0.5, 1.5, ALU.mult, ALU.add))
                link(it, stage, V.tensor_tensor(out, y, tmp, ALU.mult))

            def group_stats(it):
                st = "gn"
                if it is None:
                    dve.wait_ge(first_x, 16)
                else:
                    dve.wait_ge(xt_in, upto("xt_in", it, "gn", 0))
                for c in range(NC):
                    ins = V.bn_stats(gs6[:, c, :], xg[0:C, c * HALF:(c + 1) * HALF])
                link(it, st, ins)
                means = gs6[:, :, :].rearrange("p c (k s) -> p (c k) s", s=3)[:, :, 1]
                sqs = gs6[:, :, :].rearrange("p c (k s) -> p (c k) s", s=3)[:, :, 2]
                link(it, st, V.tensor_tensor(gsm[:, 0:4], means, means, ALU.mult))
                V.reduce_sum(gst[:, 0:1], means, AX)
                V.reduce_sum(gsm[:, 4:5], gsm[:, 0:4], AX)
                link(it, st, V.reduce_sum(gsm[:, 5:6], sqs, AX))
                V.scalar_tensor_tensor(out=gst[:, 1:2], in0=gsm[:, 5:6], scalar=4.0 / T, in1=gsm[:, 4:5],
                                       op0=ALU.mult, op1=ALU.add).then_inc(gstat, 1)

            def group_norm(it):
                st = "gn"
                dve.wait_ge(gsum_full, upto("gsum_full", it, st, 1))
                V.tensor_scalar(gm[:, 0:2], psO[0:C, 0:2], 0.25, None, ALU.mult).then_inc(gsum_free, 1)
                dve.wait_ge(gsum_free, upto("gsum_free", it, st, 1))
                link(it, st, V.scalar_tensor_tensor(out=gm[:, 2:3], in0=gm[:, 0:1], scalar=gm[:, 0:1], in1=gm[:, 1:2],
                                                op0=ALU.mult, op1=ALU.subtract))
                V.tensor_scalar(gm[:, 3:4], gm[:, 2:3], -1.0, GN_EPS, ALU.mult, ALU.add).then_inc(var_ready, 1)
                newton(it, st, gm[:, 3:4], gm[:, 5:6], gm[:, 6:7], gm[:, 7:8])
                V.tensor_scalar(xg[0:C, :], xg[0:C, :], gm[:, 0:1], gm[:, 7:8], ALU.subtract,
                                ALU.mult).then_inc(xnt_gn, 1)

            def residual(it, stage, layer, s):
                n = s if layer == 0 else fills(stage, kind_of(it)).index(("qk", s))
                dve.wait_ge(lvl1, upto("lvl1", it, stage, s + 1))
                V.scalar_tensor_tensor(out=res_of[s][0:C, :], in0=psT[0:C, t_slot(stage, n), :],
                                       scalar=(1.0, SCALE)[s], in1=split[:, s, 0, :], op0=ALU.mult,
                                       op1=ALU.subtract).then_inc(t_free, 1)

            def maxima(it, layer, fills):
                st = f"attn{layer}"
                for fill in fills:
                    h, t, kc = MAX_STEPS[layer][fill]
                    dve.wait_ge(s_full, upto("s_full", it, st, fill + 1))
                    p = h // 2
                    V.reduce_max(mx[layer][:, p % 2, (h % 2) * NT + t, kc:kc + 1],
                                 psS[:, s_bank(st, fill), 0:max_cols(layer, t, kc)], AX).then_inc(s_free, 1)
                    if (fill + 1) % PER_PAIR[layer] == 0:
                        dve.wait_ge(s_free, upto("s_free", it, st, fill + 1))
                        dve.wait_ge(m_full, upto("m_full", it, st, p - 1))
                        V.tensor_tensor(mrow[:, p % 2, :], mx[layer][:, p % 2, :, 0], mx[layer][:, p % 2, :, 1],
                                        ALU.max).then_inc(rowmax, 1)

            def den(it, st):
                dve.wait_ge(il0, upto("il0", it, st, 1))
                link(it, st, V.tensor_tensor(lb[:, :], lb[:, :], il[:, :], ALU.mult))
                link(it, st, V.scalar_tensor_tensor(out=il[:, :], in0=lb[:, :], scalar=2.0, in1=il[:, :],
                                                op0=ALU.subtract, op1=ALU.mult))
                V.scalar_tensor_tensor(out=att[0:C, :], in0=il[:, :], scalar=-1.0, in1=au[:, :], op0=ALU.mult,
                                       op1=ALU.mult).then_inc(att_ready, 1)

            def res(it, st, layer):
                old, new = ((x0, x1), (x1, x2))[layer]
                new_b, old_b = (x[:, :, :].rearrange("p (b t) c -> p b (t c)", b=NC) for x in (new, old))
                if layer == 0:
                    dve.wait_ge(x0_in, upto("x0_in", it, st, 0))
                    n = fills(st, kind_of(it)).index(("res", layer))
                    dve.wait_ge(t_full, upto("t_full", it, st, n + 1))
                    o = psT[:, t_slot(st, n), :].rearrange("p (b r) -> p b r", b=NC)[:, :, 0:4 * C]
                    V.tensor_tensor(new_b, o, old_b, ALU.add).then_inc(t_free, 1)
                    freed = len([f for f in fills(st, kind_of(it))[:n + 1] if not by_act(f)])
                    dve.wait_ge(t_free, upto("t_free", it, st, freed))
                else:
                    dve.wait_ge(out_done, upto("out_done", it, st, 0))
                    for b in range(NC):
                        dve.wait_ge(s_full, upto("s_full", it, st, b + 1))
                        V.tensor_tensor(new_b[:, b], psS[:, b, 0:4 * C], old_b[:, b], ALU.add).then_inc(s_free, 1)
                    dve.wait_ge(s_free, upto("s_free", it, st, 2))
                for t in range(NT):
                    ins = V.bn_stats(st6[:, t, :], new[:, t, :])
                link(it, st, ins)
                me, ve, mo, vo = (st6[:, :, k] for k in (1, 2, 4, 5))
                V.tensor_tensor(sm[:, 0, :], me, mo, ALU.add)
                V.tensor_tensor(sm[:, 1, :], me, mo, ALU.subtract)
                link(it, st, V.tensor_tensor(sm[:, 2, :], ve, vo, ALU.add))
                V.tensor_scalar(sm[:, 8, :], sm[:, 0, :], 0.5, None, ALU.mult)
                link(it, st, V.scalar_tensor_tensor(out=sm[:, 3, :], in0=sm[:, 1, :], scalar=0.25, in1=sm[:, 1, :],
                                                op0=ALU.mult, op1=ALU.mult))
                link(it, st, V.scalar_tensor_tensor(out=sm[:, 4, :], in0=sm[:, 2, :], scalar=1.0 / C, in1=sm[:, 3, :],
                                                op0=ALU.mult, op1=ALU.add))
                V.tensor_scalar(sm[:, 5, :], sm[:, 4, :], LN_EPS, None, ALU.add).then_inc(var_ready, 1)

            def nrm(it, st, layer):
                new = (x1, x2)[layer]
                newton(it, st, sm[:, 5, :], sm[:, 7, :], sm[:, 9, :], sm[:, 10, :])
                for t in range(NT):
                    ins = V.tensor_scalar(xn_tok[:, t, :], new[:, t, :], sm[:, 8, t:t + 1], sm[:, 10, t:t + 1],
                                          ALU.subtract, ALU.mult)
                ins.then_inc(xn_tok_ready, 1)

            def gates(it):
                st = "mix"
                dve.wait_ge(m_full, upto("m_full", it, st, 1))
                s = psM[:, 0:NT * NE].rearrange("p (t x) -> p t x", x=NE)

                def over(row):
                    return row.unsqueeze(2).to_broadcast([P, NT, NE])

                link(it, st, V.reduce_max(gden[:, 0, :], s, AX))
                V.tensor_tensor(g4[:, 0], s, over(gden[:, 0, :]), ALU.subtract).then_inc(gate_max_ready, 1)
                dve.wait_ge(gate_exp_ready, upto("gate_exp_ready", it, st, 1))
                link(it, st, V.reduce_sum(gden[:, 1, :], g4[:, 1], AX))
                link(it, st, V.reciprocal(gden[:, 2, :], gden[:, 1, :]))
                link(it, st, V.tensor_tensor(g4[:, 2], g4[:, 1], over(gden[:, 2, :]), ALU.mult))
                shape = [P, NT, NE, NE]
                mine = g4[:, 2].unsqueeze(3).to_broadcast(shape)
                other = g4[:, 2].unsqueeze(2).to_broadcast(shape)
                V.tensor_tensor(g16[:, 0], other, mine, ALU.is_gt)
                link(it, st, V.tensor_tensor(g16[:, 1], other, mine, ALU.is_equal))
                tie = cst[:, C_TIE:C_TIE + NE * NE].rearrange("p (i j) -> p i j", j=NE).unsqueeze(1).to_broadcast(shape)
                link(it, st, V.tensor_tensor(g16[:, 1], g16[:, 1], tie, ALU.mult))
                link(it, st, V.tensor_tensor(g16[:, 0], g16[:, 0], g16[:, 1], ALU.add))
                link(it, st, V.reduce_sum(g4[:, 3], g16[:, 0], AX))
                link(it, st, V.scalar_tensor_tensor(out=g4[:, 4], in0=g4[:, 3], scalar=1.5, in1=g4[:, 2],
                                                op0=ALU.is_lt, op1=ALU.mult))
                link(it, st, V.reduce_sum(gden[:, 0, :], g4[:, 4], AX))
                link(it, st, V.tensor_scalar(gden[:, 1, :], gden[:, 0, :], GATE_EPS, None, ALU.add))
                link(it, st, V.reciprocal(gden[:, 2, :], gden[:, 1, :]))
                V.tensor_tensor(g4[:, 0], g4[:, 4], over(gden[:, 2, :]), ALU.mult).then_inc(m_free, 1)

            def first_maxima(it, st, n):
                fill, layer = fills(st, kind_of(it)).index(("max", n)), 0 if st == "turn" else 1
                cols = T if layer == 0 else (n % NT + 1) * P
                if n == 0:
                    dve.wait_ge(m_full, upto("m_full", it, st, 0))
                dve.wait_ge(t_full, upto("t_full", it, st, fill + 1))
                V.reduce_max(mrow[:, 0, n:n + 1], psT[:, t_slot(st, fill), 0:cols], AX).then_inc(t_free, 1)

            def expert_add(it, stage, x):
                i = x - first_expert(stage)
                dve.wait_ge(y_full, upto("y_full", it, stage, i + 1))
                dve.wait_ge(y_free, upto("y_free", it, stage, i))
                for t in range(NT):
                    y = psOM[:, t // 4, (t % 4) * C:(t % 4 + 1) * C]
                    ins = V.scalar_tensor_tensor(out=x2[:, t, :], in0=y, scalar=g4[:, 0, t, x:x + 1],
                                                 in1=x2[:, t, :], op0=ALU.mult, op1=ALU.add)
                ins.then_inc(y_free, 1)

            def norm(it):
                res(it, "norm", 1)
                nrm(it, "norm", 1)
                for b in range(NC):
                    dve.wait_ge(s_full, upto("s_full", it, "norm", 2 + b + 1))
                    V.tensor_copy(xf[0:C, b * HALF:(b + 1) * HALF], psS[0:C, b, :]).then_inc(s_free, 1)

            def turn(it):
                for what, n in steps("turn", kind_of(it)):
                    if what == "back":
                        expert_add(it, "turn", n)
                    elif what == "rel":
                        o = psT[:, t_slot("turn", fills("turn", kind_of(it)).index((what, n))), :]
                        views = zip(rel_views(qa, 64, n, o), rel_views(qb, 0, n, o))
                        for i, (lead, rest) in enumerate(views):
                            dve.wait_ge(rel_lead, upto("rel_lead", it, "turn", 2 * n + i + 1))
                            ins = V.tensor_tensor(rest[0], rest[1], lead[0], ALU.subtract)
                        ins.then_inc(t_free, 1)
                    elif what == "max":
                        first_maxima(it, "turn", n)

            def mix(it):
                st = "mix"
                if it is not None:
                    gates(it)
                    dve.wait_ge(m_free, upto("m_free", it, st, 1))
                for what, n in steps(st, kind_of(it)):
                    if what == "back":
                        expert_add(it, st, n)
                    elif what == "den":
                        den(it, st)
                    elif what == "res":
                        res(it, st, n)
                    elif what == "nrm":
                        nrm(it, st, n)
                    elif what == "qk":
                        residual(it, st, 1, n)
                    elif what == "lev":
                        dve.wait_ge(lvl2, upto("lvl2", it, st, 2))
                        V.tensor_tensor(split[:, 1, 2, :], res_of[1][0:C, :], split[:, 1, 1, :],
                                        ALU.subtract).then_inc(lvl3_k1, 1)
                    elif what == "max":
                        first_maxima(it, st, n)

            def attention1(it):
                per = PER_PAIR[1]
                if kind_of(it) in ("second", "body"):
                    group_stats(it)
                    maxima(it, 1, range(LEAD))
                    group_norm(it)
                    maxima(it, 1, range(LEAD, per + 2))
                    for s in range(2):
                        residual(it, "qkv0", 0, s)
                    maxima(it, 1, range(per + 2, 2 * per))
                else:
                    maxima(it, 1, range(2 * per))

            group_stats(None)
            group_norm(None)
            for s in range(2):
                residual(None, "qkv0", 0, s)
            turn(None)
            maxima(None, 0, range(len(MAX_STEPS[0])))
            mix(None)
            attention1(0)
            turn(0)
            maxima(0, 0, range(len(MAX_STEPS[0])))
            norm(0)
            mix(0)
            with dve.Fori(1, B - 1) as it:
                attention1(it)
                turn(it)
                maxima(it, 0, range(len(MAX_STEPS[0])))
                norm(it)
                mix(it)
            attention1(B - 1)
            turn(B - 1)
            norm(B - 1)
            mix(B - 1)
            for (kind, stage), n in count.items():
                assert incs("dve_chain", stage, kind) == n, (stage, kind, n)




def _constants(np):
    c = np.zeros((P, C_END), np.float32)
    i, j = np.arange(P)[:, None], np.arange(P)[None, :]
    c[:, C_ID:C_ID + P] = i == j
    g = np.arange(C) // GROUP
    c[0:C, C_GRP:C_GRP + C] = (g[:, None] == g[None, :]) / GROUP
    x = np.arange(NE)
    c[:, C_TIE:C_TIE + NE * NE] = (x[None, :] < x[:, None]).reshape(1, -1)
    level = np.repeat(K_SLOTS, HD)
    c[0:C, C_S1] = np.where(level >= 1, -1, 0)
    c[0:C, C_S2] = np.where(level >= 2, -1, 0)
    return c


def _hots(np):
    key = np.arange(T)
    return np.concatenate([key[None, :] // WS == np.arange(HS)[:, None],
                           key[None, :] % WS == np.arange(WS)[:, None]]).astype(np.float32)


def _masks(np):
    i, j = np.arange(P)[:, None], np.arange(P)[None, :]
    return np.concatenate([np.where(j > i, -BIG, 0), np.where(i > j, -BIG, 0)], 1).astype(np.float32)


def kernel(x, L0_conv_qkv_w, L0_conv_qkv_b, L0_conv_proj_w, L0_conv_proj_b, L0_conv_rel_pos_h, L0_conv_rel_pos_w,
           L1_attn_w_attn, L1_attn_w_proj, L1_ffn_gate_w, L1_ffn_gate_b, L1_ffn_w1, L1_ffn_b1, L1_ffn_w2, L1_ffn_b2):
    import numpy as np
    import concourse.bacc as bacc
    from concourse.bass_utils import run_bass_kernel_spmd as run

    def table(r):
        return np.tile(np.asarray(r)[::-1].T, (len(K_SLOTS), 1))

    x = np.asarray(x)
    arrays = {
        "x_tok": x.reshape(B, NT, P, C).transpose(0, 2, 1, 3),
        "x_t": np.concatenate([x, x[:1]]).reshape(B + 1, T, C).transpose(0, 2, 1),

        "consts": _constants(np), "hots": _hots(np), "masks": _masks(np),
        "w_qkv0": L0_conv_qkv_w, "b_qkv0": np.asarray(L0_conv_qkv_b)[None, :],
        "w_p0": L0_conv_proj_w, "b_p0": np.asarray(L0_conv_proj_b)[None, :],
        "rel_h": table(L0_conv_rel_pos_h), "rel_w": table(L0_conv_rel_pos_w),
        "w_qkv1": L1_attn_w_attn, "w_p1": L1_attn_w_proj,
        "gate_w": L1_ffn_gate_w, "gate_b": np.asarray(L1_ffn_gate_b)[None, :],
        "w1": L1_ffn_w1, "b1": np.asarray(L1_ffn_b1).reshape(1, -1),
        "w2": L1_ffn_w2, "b2": np.asarray(L1_ffn_b2).T,
    }
    arrays = {n: np.ascontiguousarray(a) for n, a in arrays.items()}
    nc = bacc.Bacc("TRN2", target_bir_lowering=False, num_devices=1)
    args = [nc.dram_tensor(n, a.shape, mybir.dt.from_np(a.dtype), kind="ExternalInput").ap()
            for n, a in arrays.items()]
    out = nc.dram_tensor("out", (B, P, NT, C), F32, kind="ExternalOutput").ap()
    build(nc, *args, out)
    r = run(nc, [arrays], core_ids=[0])
    got = np.asarray(r.results[0]["out"])
    return np.ascontiguousarray(got.transpose(0, 2, 1, 3)).reshape(B, HS, WS, C)
```
